# Optimizing a Trainium2 kernel written in Bass

```python
import numpy as np
import jax
import jax.numpy as jnp

def _softmax(x, axis=-1):
    return jax.nn.softmax(x, axis=axis)
def _gelu(x):
    return jax.nn.gelu(x, approximate=True)
def _silu(x):
    return jax.nn.silu(x)
def _sigmoid(x):
    return jax.nn.sigmoid(x)
def _layernorm(x, axis=-1, eps=1e-5):
    m = jnp.mean(x, axis=axis, keepdims=True)
    v = jnp.var(x, axis=axis, keepdims=True)
    return (x - m) / jnp.sqrt(v + eps)
def _scatter_add(tgt, idx, src, axis=0):
    return tgt.at[idx].add(src)
def _segment_sum(src, seg, n):
    return jax.ops.segment_sum(src, seg, n)

kernel_name = 'mk_conv_seq_d1_conv_nchw256_4ab26d'

def setup_inputs(seed: int = 0):
    np.random.seed(seed)
    _w = jnp.asarray
    def _rec_inputs():
        import jax
        import jax.numpy as jnp
        _gk = jax.random.key(seed)
        x = -7.109e-05 + 0.9999 * jax.random.normal(jax.random.fold_in(_gk, 1), (16, 256, 128, 128), jnp.float32)
        return x
    x = _rec_inputs()
    def _L0_conv_setup():
        import jax, jax.numpy as jnp
        import numpy as np
        EPS = 1e-05

        def _zpool(z):
            return jnp.stack([z.max(axis=1), z.mean(axis=1)], axis=1)

        def _conv7(z, w, b):
            y = jax.lax.conv_general_dilated(z, w, window_strides=(1, 1), padding=[(3, 3), (3, 3)], dimension_numbers=('NCHW', 'OIHW', 'NCHW'))
            return y + b.reshape(1, -1, 1, 1)

        def _gate(z, w, b):
            return jax.nn.sigmoid(_conv7(_zpool(z), w, b))
        key = jax.random.key(seed)
        ks = jax.random.split(key, 8)
        N, C, H, W = (16, 256, 128, 128)
        x = jax.random.normal(ks[0], (N, C, H, W), dtype=jnp.float32)
        bn_w = jnp.ones((C,), dtype=jnp.float32)
        bn_b = jnp.zeros((C,), dtype=jnp.float32)

        def convp(k):
            kw, kb = jax.random.split(k)
            w = jax.random.normal(kw, (1, 2, 7, 7), dtype=jnp.float32) * 0.05
            b = jax.random.normal(kb, (1,), dtype=jnp.float32) * 0.05
            return (w, b)
        wH, bH = convp(ks[1])
        wW, bW = convp(ks[2])
        wS, bS = convp(ks[3])
        gamma = jnp.float32(0.1)
        return {'x': x, 'bn_w': bn_w, 'bn_b': bn_b, 'wH': wH, 'bH': bH, 'wW': wW, 'bW': bW, 'wS': wS, 'bS': bS, 'gamma': gamma}
    _L0_conv_all = _L0_conv_setup()
    _L0_conv_in = {k: v for k, v in _L0_conv_all.items() if k in ('bn_w', 'bn_b', 'wH', 'bH', 'wW', 'bW', 'wS', 'bS', 'gamma', )}
    del _L0_conv_all

    return {
        "x": x,
        "L0_conv_bn_w": _L0_conv_in["bn_w"],
        "L0_conv_bn_b": _L0_conv_in["bn_b"],
        "L0_conv_wH": _L0_conv_in["wH"],
        "L0_conv_bH": _L0_conv_in["bH"],
        "L0_conv_wW": _L0_conv_in["wW"],
        "L0_conv_bW": _L0_conv_in["bW"],
        "L0_conv_wS": _L0_conv_in["wS"],
        "L0_conv_bS": _L0_conv_in["bS"],
        "L0_conv_gamma": _L0_conv_in["gamma"],
    }

def reference(x, L0_conv_bn_w, L0_conv_bn_b, L0_conv_wH, L0_conv_bH, L0_conv_wW, L0_conv_bW, L0_conv_wS, L0_conv_bS, L0_conv_gamma):
    import jax
    import jax.numpy as jnp
    def _L0_conv_ref(x, bn_w, bn_b, wH, bH, wW, bW, wS, bS, gamma):
        import jax, jax.numpy as jnp
        import numpy as np
        EPS = 1e-05

        def _zpool(z):
            return jnp.stack([z.max(axis=1), z.mean(axis=1)], axis=1)

        def _conv7(z, w, b):
            y = jax.lax.conv_general_dilated(z, w, window_strides=(1, 1), padding=[(3, 3), (3, 3)], dimension_numbers=('NCHW', 'OIHW', 'NCHW'))
            return y + b.reshape(1, -1, 1, 1)

        def _gate(z, w, b):
            return jax.nn.sigmoid(_conv7(_zpool(z), w, b))
        mean = x.mean(axis=(0, 2, 3), keepdims=True)
        var = x.var(axis=(0, 2, 3), keepdims=True)
        x_norm = (x - mean) * jax.lax.rsqrt(var + EPS)
        x_norm = x_norm * bn_w.reshape(1, -1, 1, 1) + bn_b.reshape(1, -1, 1, 1)
        x1 = jnp.transpose(x_norm, (0, 2, 1, 3))
        o1 = jnp.transpose(_gate(x1, wH, bH) * x1, (0, 2, 1, 3))
        x2 = jnp.transpose(x_norm, (0, 3, 2, 1))
        o2 = jnp.transpose(_gate(x2, wW, bW) * x2, (0, 3, 2, 1))
        o3 = _gate(x_norm, wS, bS) * x_norm
        out = (o1 + o2 + o3) / 3.0
        return x + gamma * out

    def _gn(v, G=32, eps=1e-5):
        B_, C_, H_, W_ = v.shape
        g = v.reshape(B_, G, C_ // G, H_, W_)
        m = jnp.mean(g, axis=(2, 3, 4), keepdims=True)
        s = jnp.var(g, axis=(2, 3, 4), keepdims=True)
        return ((g - m) / jnp.sqrt(s + eps)).reshape(v.shape)

    def _ln_c(v, eps=1e-6):
        m = jnp.mean(v, axis=1, keepdims=True)
        s = jnp.var(v, axis=1, keepdims=True)
        return (v - m) / jnp.sqrt(s + eps)

    def _ln_t(v, eps=1e-5):
        m = jnp.mean(v, axis=-1, keepdims=True)
        s = jnp.var(v, axis=-1, keepdims=True)
        return (v - m) / jnp.sqrt(s + eps)

    def _to_tokens(v):
        B_, C_, H_, W_ = v.shape
        return v.reshape(B_, C_, H_ * W_).transpose(0, 2, 1)
    def _from_tokens(t, like):
        B_, C_, H_, W_ = like.shape
        return t.transpose(0, 2, 1).reshape(B_, C_, H_, W_)

    x = _L0_conv_ref(x, L0_conv_bn_w, L0_conv_bn_b, L0_conv_wH, L0_conv_bH, L0_conv_wW, L0_conv_bW, L0_conv_wS, L0_conv_bS, L0_conv_gamma)
    return x


_drawn_inputs = setup_inputs


def setup_inputs(seed=0):
    import zlib

    import numpy as np

    out = dict(_drawn_inputs(seed))
    spreads = {'L0_conv_bn_w': (1.0, 0.6), 'L0_conv_bn_b': (0.0, 0.8)}
    factors = {'L0_conv_wH': 8.0, 'L0_conv_wW': 22.257, 'L0_conv_wS': 64.0}
    for name, (base, spread) in spreads.items():
        noise = np.random.default_rng([zlib.crc32(name.encode()), seed]).standard_normal(out[name].shape)
        drawn = base * np.exp(spread * noise) if base else spread * noise
        out[name] = jnp.asarray(drawn.astype(out[name].dtype))
    for name, factor in factors.items():
        out[name] = (out[name] * factor).astype(out[name].dtype)
    return out
```

```python
from contextlib import ExitStack

import concourse.bass as bass
from concourse import mybir

F32 = mybir.dt.float32
BF16 = mybir.dt.bfloat16
ALU = mybir.AluOpType
ACT = mybir.ActivationFunctionType
AX = mybir.AxisListType

BN_EPS = 1e-5
TAPS = 7
PAD = TAPS // 2


def triple_gate_kernel(nc, x, bn_w, bn_b, w_h, b_h, w_w, b_w, w_s, b_s, gamma, out):
    N, C, H, W = x.shape
    P = 128
    HALVES = C // P
    ROWS = 16
    TILES = H // ROWS
    TPX = ROWS * W
    QROWS = 4
    QUADS = ROWS // QROWS
    QPX = QROWS * W
    SROWS = 8
    STRIPS = ROWS // SROWS
    SPX = SROWS * W
    UNITS = STRIPS * HALVES
    PARTS = 3
    GROW = PARTS * ROWS
    KROWS = GROW + PARTS
    LAG = 2
    assert HALVES == STRIPS == 2 and H == W == P and KROWS <= P

    with ExitStack() as ctx:
        def sb(name, shape, dt=F32):
            return ctx.enter_context(nc.sbuf_tensor(name, shape, dt))

        def pb(name, shape):
            return ctx.enter_context(nc.psum_tensor(name, shape, F32))

        def sem(name):
            return ctx.enter_context(nc.semaphore(name))

        image = sb("image", [P, TILES, HALVES, TPX])
        normed = sb("normed", [P, 2, HALVES, QPX])
        halfmax = sb("halfmax", [P, 2, QPX])
        scaled = sb("scaled", [P, 2, SPX])
        csum_row = sb("csum_row", [P, 2, QUADS * W])
        bands = sb("bands", [P, 3, 2 * TAPS, P])
        pix = sb("pix", [P, 2, TPX], BF16)
        gw_stack = sb("gw_stack", [P, TILES, C], BF16)
        z_h = sb("z_h", [P, 2, C + 2 * PAD])
        z_w = sb("z_w", [P, 2, C + 2 * PAD])
        z_s = sb("z_s", [P, 2, W + 2 * PAD])
        gate_h = sb("gate_h", [P, C])
        gate_w = sb("gate_w", [P, C])
        gate_s = sb("gate_s", [P, W])
        gate_w_parts = sb("gate_w_parts", [P, PARTS, C], BF16)
        gate_s_parts = sb("gate_s_parts", [P, PARTS, W], BF16)
        pools = sb("pools", [P, 3, C])
        wmax = sb("wmax", [P, HALVES, H])
        cmax_t = sb("cmax_t", [P, H])
        ident = sb("ident", [P, P])
        CONSTS = 9 + TAPS + 2 * PARTS
        BANDS = 3 * (2 * TAPS + TAPS - 1)
        VAR_STEPS, STAT_STEPS = 6, 17
        mean_col = sb("mean_col", [P, 32])
        a_row = sb("a_row", [P, 4, P])
        a_row_w = sb("a_row_w", [P, C])
        wts = sb("wts", [P, 3, 2 * TAPS * TAPS])
        small = sb("small", [P, 64])
        squares = sb("squares", [P, N, TILES, HALVES])
        totals = sb("totals", [P, N, HALVES])
        run_max = normed[:, :, :, :].rearrange("p a b x -> p (a b x)").rearrange("p (f x) -> p f x", f=HALVES)
        folded = scaled[:, :, :].rearrange("p b (f r w) -> p b f r w", f=HALVES, w=W // 2)
        square_junk = halfmax[:, :, :].rearrange("p a x -> p (a x)").bitcast(BF16)
        hmax = csum_row[:, 0, 0:HALVES * W].rearrange("p (f w) -> p f w", f=HALVES)
        hmax_raw = csum_row[:, 1, 0:HALVES * W].rearrange("p (f w) -> p f w", f=HALVES)
        wsum = wmax
        band_step = pix[:, :, :].rearrange("p a x -> p (a x)").bitcast(F32)[:, 0:2 * TAPS * P].rearrange(
            "p (t q) -> p t q", q=P)
        diagonals = gw_stack[:, :, :].rearrange("p a x -> p (a x)").bitcast(F32)[:, 0:TAPS * P].rearrange(
            "p (k q) -> p k q", q=P)

        (SIGN, A, D, A3, D3, BNW, BNB, G3, BIAS, MEAN, VAR, RSTD, T0, T1, T2) = (4 * i for i in range(15))
        col = lambda n, f=0, k=1: small[:, n + f:n + f + k]

        gates_ps = [pb("gates_ps0", [P, SPX]), pb("gates_ps1", [P, SPX])]
        turn_ps = [pb("turn_ps0", [P, QPX]), pb("turn_ps1", [P, QPX])]
        csum_ps = pb("csum_ps", [P, QUADS * W])
        conv_ps = pb("conv_ps", [P, C])

        kept = nc.dram_tensor("kept_pools", (N, P, 3, C), F32, kind="Internal").ap()
        via_w = nc.dram_tensor("via_w", (H, PARTS, C), BF16, kind="Internal").ap()
        via_s = nc.dram_tensor("via_s", (H, PARTS, W), BF16, kind="Internal").ap()
        via_s_t = via_s.rearrange("(t r) a w -> t a r w", r=ROWS)

        x_t = x.rearrange("n (f p) (t r) w -> n t p f (r w)", p=P, r=ROWS)
        out_t = out.rearrange("n (f p) (t r) w -> n t p f (r w)", p=P, r=ROWS)

        loaded = [sem(f"loaded{k}") for k in range(TILES)]
        stored = [sem(f"stored{k}") for k in range(TILES)]
        params = sem("params")
        consts = sem("consts")
        signed = sem("signed")
        band_done = sem("band_done")
        squared = sem("squared")
        max_step = sem("max_step")
        fold_ready = sem("fold_ready")
        fold_used = sem("fold_used")
        h_summed = sem("h_summed")
        h_maxed = sem("h_maxed")
        pools_ready = sem("pools_ready")
        pools_turned = sem("pools_turned")
        pools_out = sem("pools_out")
        pools_kept = sem("pools_kept")
        pools_in = sem("pools_in")
        stat = sem("stat")
        rooted = sem("rooted")
        rows_turned = sem("rows_turned")
        rows_out = sem("rows_out")
        z_scaled = sem("z_scaled")
        z_pooled = sem("z_pooled")
        normed_ready = sem("normed_ready")
        half_ready = sem("half_ready")
        c_summed = sem("c_summed")
        turned = sem("turned")
        c_maxed = sem("c_maxed")
        csum_out = sem("csum_out")
        csum_in = [sem("csum_in0"), sem("csum_in1")]
        h_conv = sem("h_conv")
        w_conv = sem("w_conv")
        s_conv = sem("s_conv")
        h_gate = sem("h_gate")
        w_gate = sem("w_gate")
        s_gate = sem("s_gate")
        w_turned = sem("w_turned")
        c_turned = sem("c_turned")
        z_w_ready = sem("z_w_ready")
        z_s_ready = sem("z_s_ready")
        w_split_step = sem("w_split_step")
        s_split_step = sem("s_split_step")
        w_left = sem("w_left")
        s_left = sem("s_left")
        w_stacked = sem("w_stacked")
        s_rows = [sem("s_rows0"), sem("s_rows1")]
        gates_ready = sem("gates_ready")
        scaled_ready = sem("scaled_ready")
        gated = sem("gated")
        added = sem("added")
        SPLIT = 2 * PARTS - 1

        block = ctx.enter_context(nc.Block())

        def tile(n, k):
            return n * TILES + k

        def quad(m, k, q):
            return m * (TILES * QUADS) + (k * QUADS + q)

        def unit(j, k, u):
            return j * (TILES * UNITS) + (k * UNITS + u)

        @block.sync
        def _(sp):
            for g, src in enumerate((w_h, w_w, w_s)):
                flat = src.rearrange("o i a b -> o (i a b)")
                sp.dma_start(wts[:, g, :], flat.to_broadcast([P, 2 * TAPS * TAPS])).then_inc(params, 16)
            for g, src in enumerate((b_h, b_w, b_s, gamma)):
                at = BIAS + g if g < 3 else G3
                sp.dma_start(small[:, at:at + 1], src.to_broadcast([P, 1])).then_inc(params, 16)
            with nc.allow_non_contiguous_dma(reason="two columns of batch-norm parameters"):
                sp.dma_start(col(BNW, 0, 2), bn_w.rearrange("(f p) -> p f", p=P)).then_inc(params, 16)
                sp.dma_start(col(BNB, 0, 2), bn_b.rearrange("(f p) -> p f", p=P)).then_inc(params, 16)

            for k in range(TILES):
                sp.dma_start(image[:, k], x_t[0, k]).then_inc(loaded[k], 16)
            with sp.Fori(1, N) as n:
                for k in range(TILES):
                    halves_done = tile(n - 1, k + 1) * HALVES
                    sp.wait_ge(squared, halves_done)
                    sp.wait_ge(max_step, halves_done)
                    sp.wait_ge(fold_ready, halves_done)
                    sp.wait_ge(h_summed, halves_done)
                    sp.dma_start(image[:, k], x_t[n, k]).then_inc(loaded[k], 16)

            sp.wait_ge(pools_kept, 16 * N)
            sp.dma_start(pools[:, :, :], kept[N - 1]).then_inc(pools_in, 16)
            sp.wait_ge(consts, CONSTS)

            def spread_gate_s(k):
                rows = pix[GROW:GROW + PARTS, k % 2, :].rearrange("a (r w) -> a r w", w=W)
                sp.dma_start(rows, via_s_t[k]).then_inc(s_rows[k % 2], 16)

            def place_gates(m):
                sp.wait_ge(w_split_step, (m + 1) * SPLIT)
                sp.dma_start(via_w, gate_w_parts[:, :, :]).then_inc(w_left, 16)
                sp.wait_ge(w_left, 16 * (m + 1))
                for part in range(PARTS):
                    sp.dma_start(gw_stack[part * ROWS:(part + 1) * ROWS, :, :],
                                 via_w.rearrange("(t r) a c -> a r t c", r=ROWS)[part]).then_inc(w_stacked, 16)
                sp.wait_ge(s_split_step, (m + 1) * SPLIT)
                sp.dma_start(via_s, gate_s_parts[:, :, :]).then_inc(s_left, 16)
                sp.wait_ge(s_left, 16 * (m + 1))
                spread_gate_s(0)
                spread_gate_s(1)

            def outputs(j, here, after):
                for k in range(TILES):
                    sp.wait_ge(added, unit(j, k + 1, 0))
                    if k + 2 < TILES:
                        spread_gate_s(k + 2)
                    sp.dma_start(out_t[here, k], image[:, k]).then_inc(stored[k], 16)
                    if after is not None and k >= 1:
                        sp.wait_ge(stored[k - 1], 16 * (j + 1))
                        sp.dma_start(image[:, k - 1], x_t[after, k - 1]).then_inc(loaded[k - 1], 16)
                if after is not None:
                    sp.wait_ge(stored[TILES - 1], 16 * (j + 1))
                    sp.dma_start(image[:, TILES - 1], x_t[after, TILES - 1]).then_inc(loaded[TILES - 1], 16)

            def step(j, here, after):
                sp.wait_ge(z_scaled, (j + 1) * 3)
                sp.dma_start(pools[:, :, :], kept[after]).then_inc(pools_in, 16)
                outputs(j, here, after)
                place_gates(j + 1)

            place_gates(0)
            step(0, N - 1, 0)
            with sp.Fori(1, N - 1) as j:
                step(j, j - 1, j)
            outputs(N - 1, N - 2, None)
            for k in range(TILES):
                sp.wait_ge(stored[k], 16 * N)

        @block.gpsimd
        def _(pool):
            pool.memset(ident[:, :], 0.0).then_inc(consts, 1)
            pool.memset(diagonals, 0.0).then_inc(consts, 1)
            pool.memset(mean_col[:, :], 1.0 / C).then_inc(consts, 1)
            for z in (z_h, z_w, z_s):
                pool.memset(z[:, :, :], 0.0).then_inc(consts, 1)
            pool.wait_ge(consts, 6)
            pool.affine_select(out=ident[:, :], in_=ident[:, :], compare_op=ALU.not_equal, fill=1.0, base=0,
                               pattern=[[-1, P]], channel_multiplier=1).then_inc(consts, 1)
            for k in range(TAPS):
                pool.affine_select(out=diagonals[:, k], in_=diagonals[:, k], compare_op=ALU.not_equal,
                                   fill=1.0, base=PAD - k, pattern=[[-1, P]], channel_multiplier=1
                                   ).then_inc(consts, 1)
            pool.wait_ge(consts, 7 + TAPS)
            pool.wait_ge(params, 16 * 9)

            def sweep1(n, first=False):
                for k in range(TILES):
                    pool.wait_ge(loaded[k], 16 * (n + 1))
                    for s in range(STRIPS):
                        if not (first and k == 0):
                            pool.wait_ge(fold_used, tile(n, k) * STRIPS + s - 1)
                        px = image[:, k, :, s * SPX:(s + 1) * SPX].rearrange("p f (r w) -> p f r w", w=W)
                        pool.tensor_tensor(folded[:, s], px[:, :, :, 0:W // 2], px[:, :, :, W // 2:W],
                                           ALU.add).then_inc(fold_ready, 1)

            sweep1(0, True)
            steps = 0
            for g in range(3):
                w3 = wts[:, g, :].rearrange("p (i a b) -> p i a b", a=TAPS, b=TAPS)
                for k in range(TAPS):
                    taps = w3[:, :, :, k] if g == 0 else w3[:, :, k, :]
                    target = bands[:, g] if k == 0 else band_step
                    for i in range(2):
                        pool.tensor_tensor(target[:, i * TAPS:(i + 1) * TAPS, :],
                                           diagonals[:, k].unsqueeze(1).to_broadcast([P, TAPS, P]),
                                           taps[:, i].unsqueeze(2).to_broadcast([P, TAPS, P]),
                                           ALU.mult).then_inc(band_done, 1)
                    steps += 2
                    pool.wait_ge(band_done, steps)
                    if k:
                        pool.tensor_tensor(bands[:, g], bands[:, g], band_step, ALU.add).then_inc(band_done, 1)
                        steps += 1
                        pool.wait_ge(band_done, steps)
            assert steps == BANDS
            with pool.Fori(1, N) as n:
                sweep1(n)
            pool.memset(pix[:, :, :], 0.0).then_inc(consts, 1)
            pool.memset(gw_stack[:, :, :], 1.0).then_inc(consts, 1)
            pool.wait_ge(consts, 9 + TAPS)
            for part in range(PARTS):
                for b in range(2):
                    rows = pix[:, b, :].rearrange("p (r w) -> p r w", w=W)
                    pool.affine_select(out=rows, in_=rows, compare_op=ALU.not_equal, fill=1.0,
                                       base=-part * ROWS, pattern=[[-1, ROWS], [0, W]], channel_multiplier=1
                                       ).then_inc(consts, 1)
                pool.wait_ge(consts, 9 + TAPS + 2 * (part + 1))
            assert 9 + TAPS + 2 * PARTS == CONSTS

            def normalise_pools(m):
                a_all = a_row[:, 0:2, :].rearrange("p a q -> p (a q)")
                d_all = a_row[:, 2:4, :].rearrange("p a q -> p (a q)")
                places = (z_h[:, 1, PAD:PAD + C], z_h[:, 0, PAD:PAD + C], z_w[:, 1, PAD:PAD + C])
                pool.wait_ge(pools_in, 16 * (m + 1))
                for n, scale in enumerate((a_row_w[:, :], a_all, a_row_w[:, :])):
                    pool.tensor_tensor(places[n], pools[:, n, :], scale, ALU.mult).then_inc(z_scaled, 1)
                pool.wait_ge(z_scaled, 3 * (m + 1))
                for z in places:
                    last = pool.tensor_tensor(z, z, d_all, ALU.add)
                last.then_inc(z_pooled, 1)

            def add_x(j, k):
                for u in range(UNITS):
                    s, f = u // HALVES, u % HALVES
                    px = image[:, k, f, s * SPX:(s + 1) * SPX]
                    pool.wait_ge(gated, unit(j, k, u) + 1)
                    pool.tensor_tensor(px, px, scaled[:, u % 2, :], ALU.add).then_inc(added, 1)

            pool.wait_ge(rows_out, 2)
            normalise_pools(0)
            with pool.Fori(0, N - 1) as j:
                for k in range(TILES):
                    add_x(j, k)
                    if k == 1:
                        pool.wait_ge(w_conv, j + 1)
                        normalise_pools(j + 1)
            for k in range(TILES):
                add_x(N - 1, k)

        @block.scalar
        def _(act):
            def sweep1(n, first=False):
                for k in range(TILES):
                    act.wait_ge(loaded[k], 16 * (n + 1))
                    for f in range(HALVES):
                        if not (first and k == 0 and f == 0):
                            act.wait_ge(squared, tile(n, k) * HALVES + f)
                        act.activation(square_junk, image[:, k, f, :], ACT.Square,
                                       accum_out=squares[:, n, k, f:f + 1]).then_inc(squared, 1)
                act.wait_ge(pools_turned, n + 1)
                if not first:
                    act.wait_ge(pools_kept, 16 * n)
                act.activation(pools[:, 0, :], conv_ps[:, :], ACT.Identity)
                act.activation(pools[:, 1:3, :].rearrange("p a c -> p (a c)"), csum_ps[:, :],
                               ACT.Identity).then_inc(pools_out, 1)
                act.wait_ge(pools_out, n + 1)
                act.dma_start(kept[n], pools[:, :, :]).then_inc(pools_kept, 16)

            sweep1(0, True)
            with act.Fori(1, N) as n:
                sweep1(n)
            act.wait_ge(stat, VAR_STEPS)
            act.activation(col(RSTD, 0, 2), col(VAR, 0, 2), ACT.Sqrt).then_inc(rooted, 1)
            act.wait_ge(stat, STAT_STEPS)

            def normalise(m, k, q, first=False):
                Q = quad(m, k, q)
                if not (first and k == 0 and q < 2):
                    act.wait_ge(half_ready, Q - 1)
                    act.wait_ge(c_summed, Q - 1)
                for f in range(HALVES):
                    last = act.activation(normed[:, q % 2, f, :], image[:, k, f, q * QPX:(q + 1) * QPX],
                                          ACT.Identity, scale=col(A, f), bias=col(D, f))
                last.then_inc(normed_ready, 1)

            def csum_leaves(m, k, first=False):
                act.wait_ge(c_summed, quad(m, k + 1, 0))
                if not (first and k < 2):
                    act.wait_ge(csum_in[k % 2], 16 * QROWS * (m * (TILES // 2) + k // 2))
                if not first and k == 0:
                    act.wait_ge(s_conv, m)
                act.activation(csum_row[:, k % 2, :], csum_ps[:, :], ACT.Identity).then_inc(csum_out, 1)
                act.wait_ge(csum_out, tile(m, k + 1))
                for row in range(QROWS):
                    h0 = k * ROWS + row
                    act.dma_start(z_s[h0:k * ROWS + ROWS:QROWS, 1, PAD:PAD + W],
                                  csum_row[32 * row:32 * row + 1, k % 2, :].rearrange(
                                      "p (q w) -> p q w", w=W)).then_inc(csum_in[k % 2], 16)

            def scale(j, k, u, first=False):
                s, f = u // HALVES, u % HALVES
                if not (first and k == 0 and u < 2):
                    act.wait_ge(added, unit(j, k, u) - 1)
                act.activation(scaled[:, u % 2, :], image[:, k, f, s * SPX:(s + 1) * SPX], ACT.Identity,
                               scale=col(A3, f), bias=col(D3, f)).then_inc(scaled_ready, 1)

            def sigmoids(m, first=False):
                act.wait_ge(h_conv, m + 1)
                if not first:
                    act.wait_ge(gates_ready, unit(m, 0, 0))
                act.activation(gate_h[:, :], conv_ps[:, :], ACT.Sigmoid, bias=col(BIAS, 0)).then_inc(h_gate, 1)
                act.wait_ge(w_conv, m + 1)
                if not first:
                    act.wait_ge(w_split_step, SPLIT * m)
                act.activation(gate_w[:, :], turn_ps[0][:, 0:C], ACT.Sigmoid, bias=col(BIAS, 1)
                               ).then_inc(w_gate, 1)
                act.wait_ge(s_conv, m + 1)
                if not first:
                    act.wait_ge(s_split_step, SPLIT * m)
                act.activation(gate_s[:, :], csum_ps[:, 0:W], ACT.Sigmoid, bias=col(BIAS, 2)
                               ).then_inc(s_gate, 1)

            def pooling(m, k, q, first=False):
                if q == 0:
                    act.wait_ge(loaded[k], 16 * (N + m))
                normalise(m, k, q, first)

            for k in range(TILES):
                for q in range(QUADS):
                    pooling(0, k, q, True)
                csum_leaves(0, k, True)
            sigmoids(0, True)

            def image_step(j, first=False):
                for k in range(TILES + LAG):
                    for u in range(UNITS):
                        if k < TILES:
                            scale(j, k, u, first)
                        if k >= LAG:
                            pooling(j + 1, k - LAG, u)
                    if k >= LAG:
                        csum_leaves(j + 1, k - LAG)
                sigmoids(j + 1)

            image_step(0, True)
            with act.Fori(1, N - 1) as j:
                image_step(j)
            for k in range(TILES):
                for u in range(UNITS):
                    scale(N - 1, k, u)

        @block.vector
        def _(dve):
            dve.wait_ge(params, 16 * 9)
            dve.tensor_scalar(col(T0, 0, 2), col(BNW, 0, 2), 0.0, None, ALU.is_ge).then_inc(signed, 1)
            dve.wait_ge(signed, 1)
            dve.tensor_scalar(col(SIGN, 0, 2), col(T0, 0, 2), 2.0, -1.0, ALU.mult, ALU.add).then_inc(signed, 1)
            dve.wait_ge(signed, 2)

            def sweep1(n, first=False):
                for k in range(TILES):
                    dve.wait_ge(loaded[k], 16 * (n + 1))
                    for s in range(STRIPS):
                        if not (first and k == 0 and s == 0):
                            dve.wait_ge(max_step, tile(n, k) * STRIPS + s)
                        if not first and k == 0 and s == 0:
                            dve.wait_ge(h_maxed, 2 * n)
                        for f in range(HALVES):
                            px = image[:, k, f, s * SPX:(s + 1) * SPX]
                            if k == 0 and s == 0:
                                op = dve.tensor_scalar(run_max[:, f], px, col(SIGN, f), None, ALU.mult)
                            else:
                                op = dve.scalar_tensor_tensor(out=run_max[:, f], in0=px, scalar=col(SIGN, f),
                                                              in1=run_max[:, f], op0=ALU.mult, op1=ALU.max)
                        op.then_inc(max_step, 1)
                    for s in range(STRIPS):
                        if not first and k == 0 and s == 0:
                            dve.wait_ge(pools_turned, n)
                        dve.wait_ge(fold_ready, tile(n, k) * STRIPS + s + 1)
                        h0 = k * ROWS + s * SROWS
                        dve.tensor_reduce(wsum[:, :, h0:h0 + SROWS], folded[:, s], AX.X, ALU.add
                                          ).then_inc(fold_used, 1)
                dve.wait_ge(max_step, tile(n, TILES) * STRIPS)
                dve.tensor_reduce(hmax_raw, run_max.rearrange("p f (r w) -> p f w r", w=W), AX.X, ALU.max
                                  ).then_inc(h_maxed, 1)
                dve.wait_ge(fold_used, tile(n, TILES) * STRIPS)
                dve.tensor_reduce(totals[:, n, :], wsum[:, :, :], AX.X, ALU.add).then_inc(h_maxed, 1)
                dve.wait_ge(h_maxed, 2 * n + 2)
                for f in range(HALVES):
                    last = dve.tensor_scalar(hmax[:, f], hmax_raw[:, f], col(SIGN, f), None, ALU.mult)
                last.then_inc(pools_ready, 1)

            sweep1(0, True)
            with dve.Fori(1, N) as n:
                sweep1(n)

            dve.wait_ge(squared, N * TILES * HALVES)
            dve.wait_ge(pools_turned, N)
            done = [0]

            def chain(op):
                done[0] += 1
                op.then_inc(stat, 1)
                dve.wait_ge(stat, done[0])

            two = lambda c: col(c, 0, 2)
            count = N * H * W
            chain(dve.tensor_reduce(two(MEAN), totals[:, :, :].rearrange("p n f -> p f n"), AX.X, ALU.add))
            chain(dve.tensor_reduce(two(VAR), squares[:, :, :, :].rearrange("p n t f -> p f (n t)"), AX.X,
                                    ALU.add))
            chain(dve.tensor_scalar(two(MEAN), two(MEAN), 1.0 / count, None, ALU.mult))
            chain(dve.tensor_tensor(two(T0), two(MEAN), two(MEAN), ALU.mult))
            chain(dve.tensor_scalar(two(VAR), two(VAR), 1.0 / count, BN_EPS, ALU.mult, ALU.add))
            chain(dve.tensor_tensor(two(VAR), two(VAR), two(T0), ALU.subtract))
            assert done[0] == VAR_STEPS
            dve.wait_ge(rooted, 1)
            chain(dve.reciprocal(two(T1), two(RSTD)))
            chain(dve.tensor_tensor(two(T2), two(T1), two(T1), ALU.mult))
            chain(dve.tensor_tensor(two(T2), two(T2), two(VAR), ALU.mult))
            chain(dve.tensor_scalar(two(T2), two(T2), -0.5, 1.5, ALU.mult, ALU.add))
            chain(dve.tensor_tensor(two(T1), two(T1), two(T2), ALU.mult))
            chain(dve.tensor_tensor(two(A), two(BNW), two(T1), ALU.mult))
            chain(dve.tensor_tensor(two(T0), two(MEAN), two(A), ALU.mult))
            chain(dve.tensor_tensor(two(D), two(BNB), two(T0), ALU.subtract))
            chain(dve.tensor_scalar(col(G3), col(G3), 1.0 / 3.0, None, ALU.mult))
            chain(dve.tensor_scalar(two(A3), two(A), col(G3), None, ALU.mult))
            chain(dve.tensor_scalar(two(D3), two(D), col(G3), None, ALU.mult))
            assert done[0] == STAT_STEPS
            dve.wait_ge(rows_turned, 1)
            dve.tensor_copy(a_row[:, :, :].rearrange("p a q -> p (a q)"), turn_ps[0][:, :]).then_inc(rows_out, 1)
            dve.tensor_scalar(a_row_w[:, :], turn_ps[0][:, 0:C], 1.0 / W, None, ALU.mult).then_inc(rows_out, 1)

            def pool_quad(m, k, q, first=False):
                Q = quad(m, k, q)
                dve.wait_ge(normed_ready, Q + 1)
                if not first and k == 0 and q == 0:
                    dve.wait_ge(w_turned, m)
                h0 = k * ROWS + q * QROWS
                dve.tensor_reduce(wmax[:, :, h0:h0 + QROWS],
                                  normed[:, q % 2].rearrange("p f (r w) -> p f r w", w=W), AX.X, ALU.max)
                if not (first and k == 0 and q < 2):
                    dve.wait_ge(turned, Q - 1)
                dve.tensor_tensor(halfmax[:, q % 2, :], normed[:, q % 2, 0, :], normed[:, q % 2, 1, :],
                                  ALU.max).then_inc(half_ready, 1)

            def cmax_quad(m, k, q, first=False):
                dve.wait_ge(turned, quad(m, k, q) + 1)
                if not first and k == 0 and q == 0:
                    dve.wait_ge(c_turned, m)
                h0 = k * ROWS + q * QROWS
                dve.tensor_reduce(cmax_t[:, h0:h0 + QROWS],
                                  turn_ps[q % 2][:, :].rearrange("p (r c) -> p r c", c=P), AX.X, ALU.max
                                  ).then_inc(c_maxed, 1)

            def gate_unit(j, k, u):
                dve.wait_ge(gates_ready, unit(j, k, u) + 1)
                dve.wait_ge(scaled_ready, unit(j, k, u) + 1)
                dve.tensor_tensor(scaled[:, u % 2, :], gates_ps[u % 2][:, :], scaled[:, u % 2, :], ALU.mult
                                  ).then_inc(gated, 1)

            def split(m, value, parts, step, n):
                for part in range(PARTS):
                    dve.tensor_copy(parts[:, part, :], value).then_inc(step, 1)
                    if part + 1 < PARTS:
                        dve.wait_ge(step, SPLIT * m + 2 * part + 1)
                        dve.tensor_tensor(value, value, parts[:, part, :], ALU.subtract).then_inc(step, 1)
                        dve.wait_ge(step, SPLIT * m + 2 * part + 2)

            def gates(m, first=False):
                dve.wait_ge(w_turned, m + 1)
                if not first:
                    dve.wait_ge(w_conv, m)
                dve.tensor_copy(z_w[:, 0, PAD:PAD + C], turn_ps[0][:, 0:C]).then_inc(z_w_ready, 1)
                dve.wait_ge(c_turned, m + 1)
                if not first:
                    dve.wait_ge(s_conv, m)
                dve.tensor_copy(z_s[:, 0, PAD:PAD + W], turn_ps[1][:, 0:W]).then_inc(z_s_ready, 1)
                dve.wait_ge(w_gate, m + 1)
                if not first:
                    dve.wait_ge(w_left, 16 * m)
                split(m, gate_w[:, :], gate_w_parts, w_split_step, C)
                dve.wait_ge(s_gate, m + 1)
                if not first:
                    dve.wait_ge(s_left, 16 * m)
                split(m, gate_s[:, :], gate_s_parts, s_split_step, W)

            for k in range(TILES):
                for q in range(QUADS):
                    pool_quad(0, k, q, True)
                    cmax_quad(0, k, q, True)
            gates(0, True)
            with dve.Fori(0, N - 1) as j:
                for k in range(TILES + LAG):
                    for u in range(UNITS):
                        if k >= LAG:
                            pool_quad(j + 1, k - LAG, u)
                        if k < TILES:
                            gate_unit(j, k, u)
                        if k >= LAG:
                            cmax_quad(j + 1, k - LAG, u)
                gates(j + 1)
            for k in range(TILES):
                for u in range(UNITS):
                    gate_unit(N - 1, k, u)

        @block.tensor
        def _(pe):
            pe.wait_ge(consts, 7)

            def turn(dst, src, start=True, stop=True):
                return pe.matmul(dst, src, ident[:, :], start=start, stop=stop, is_transpose=True,
                                 skip_group_check=True)

            def sweep1(n, first=False):
                for k in range(TILES):
                    pe.wait_ge(loaded[k], 16 * (n + 1))
                    if not first and k == 0:
                        pe.wait_ge(pools_out, n)
                    for f in range(HALVES):
                        for r in range(ROWS):
                            last = turn(conv_ps[:, f * P:(f + 1) * P], image[:, k, f, r * W:(r + 1) * W],
                                        start=(k == 0 and f == 0 and r == 0),
                                        stop=(k == TILES - 1 and r == ROWS - 1))
                        last.then_inc(h_summed, 1)
                pe.wait_ge(pools_ready, n + 1)
                for f in range(HALVES):
                    turn(csum_ps[:, f * P:(f + 1) * P], hmax[:, f])
                for f in range(HALVES):
                    last = turn(csum_ps[:, C + f * P:C + (f + 1) * P], wsum[:, f])
                last.then_inc(pools_turned, 1)

            sweep1(0, True)
            with pe.Fori(1, N) as n:
                sweep1(n)

            pe.wait_ge(stat, STAT_STEPS)
            for i, c in enumerate((A, A + 1, D, D + 1)):
                last = pe.matmul(turn_ps[0][:, i * P:(i + 1) * P], small[:, c:c + 1].to_broadcast([P, P]),
                                 ident[:, :], start=True, stop=True)
            last.then_inc(rows_turned, 1)
            pe.wait_ge(rows_out, 2)
            pe.wait_ge(band_done, BANDS)

            def pool_quad(m, k, q, first=False):
                Q = quad(m, k, q)
                pe.wait_ge(normed_ready, Q + 1)
                if q == 0 and not (first and k == 0):
                    pe.wait_ge(csum_out, tile(m, k))
                if q == 0 and not first and k == 0:
                    pe.wait_ge(s_gate, m)
                for f in range(HALVES):
                    for r in range(QROWS):
                        last = pe.matmul(csum_ps[32 * r:32 * (r + 1), q * W:(q + 1) * W], mean_col[:, :],
                                         normed[:, q % 2, f, r * W:(r + 1) * W], start=(f == 0),
                                         stop=(f == HALVES - 1))
                last.then_inc(c_summed, 1)
                pe.wait_ge(half_ready, Q + 1)
                if not (first and k == 0 and q < 2):
                    pe.wait_ge(c_maxed, Q - 1)
                if not first and k == 0:
                    if q == 0:
                        pe.wait_ge(w_gate, m)
                    if q == 1:
                        pe.wait_ge(z_s_ready, m)
                for r in range(QROWS):
                    last = turn(turn_ps[q % 2][:, r * P:(r + 1) * P], halfmax[:, q % 2, r * W:(r + 1) * W])
                last.then_inc(turned, 1)

            def convolve(dst, g, z, width):
                for i in range(2):
                    for o in range(TAPS):
                        last = pe.matmul(dst, bands[:, g, i * TAPS + o, :], z[:, i, o:o + width],
                                         start=(i == 0 and o == 0), stop=(i == 1 and o == TAPS - 1))
                return last

            def gates(m, first=False):
                pe.wait_ge(z_pooled, m + 1)
                if not first:
                    pe.wait_ge(h_gate, m)
                convolve(conv_ps[:, :], 0, z_h, C).then_inc(h_conv, 1)
                pe.wait_ge(half_ready, quad(m + 1, 0, 0))
                pe.wait_ge(c_maxed, quad(m + 1, 0, 0))
                for f in range(HALVES):
                    last = turn(turn_ps[0][:, f * P:(f + 1) * P], wmax[:, f])
                last.then_inc(w_turned, 1)
                turn(turn_ps[1][:, 0:P], cmax_t[:, :]).then_inc(c_turned, 1)
                pe.wait_ge(z_w_ready, m + 1)
                convolve(turn_ps[0][:, 0:C], 1, z_w, C).then_inc(w_conv, 1)
                pe.wait_ge(z_s_ready, m + 1)
                pe.wait_ge(csum_out, tile(m + 1, 0))
                for b in range(2):
                    pe.wait_ge(csum_in[b], 16 * QROWS * (TILES // 2) * (m + 1))
                convolve(csum_ps[:, 0:W], 2, z_s, W).then_inc(s_conv, 1)

            def spread(j, k, u, first=False):
                s, f = u // HALVES, u % HALVES
                if k == 0 and u == 0:
                    pe.wait_ge(h_gate, j + 1)
                    pe.wait_ge(w_stacked, 16 * PARTS * (j + 1))
                if u == 0:
                    pe.wait_ge(s_rows[k % 2], 16 * (j * (TILES // 2) + k // 2 + 1))
                if not (first and k == 0 and u < 2):
                    pe.wait_ge(gated, unit(j, k, u) - 1)
                for half_strip in range(2):
                    px = s * SPX + half_strip * QPX
                    dst = gates_ps[u % 2][:, half_strip * QPX:(half_strip + 1) * QPX]
                    pe.matmul(dst, gw_stack[0:KROWS, k, f * P:(f + 1) * P], pix[0:KROWS, k % 2, px:px + QPX],
                              start=True, stop=False, skip_group_check=True)
                    for r in range(QROWS):
                        last = turn(dst[:, r * W:(r + 1) * W], gate_h[:, f * P:(f + 1) * P], start=False,
                                    stop=(r == QROWS - 1))
                last.then_inc(gates_ready, 1)

            for k in range(TILES):
                for q in range(QUADS):
                    pool_quad(0, k, q, True)
            gates(0, True)
            pe.wait_ge(consts, CONSTS)

            def image_step(j, first=False):
                for k in range(TILES + LAG):
                    for u in range(UNITS):
                        if k < TILES:
                            spread(j, k, u, first)
                        if k >= LAG:
                            pool_quad(j + 1, k - LAG, u)
                gates(j + 1)

            image_step(0, True)
            with pe.Fori(1, N - 1) as j:
                image_step(j)
            for k in range(TILES):
                for u in range(UNITS):
                    spread(N - 1, k, u)


_INS = {
    "x": "x", "bn_w": "L0_conv_bn_w", "bn_b": "L0_conv_bn_b", "w_h": "L0_conv_wH", "b_h": "L0_conv_bH",
    "w_w": "L0_conv_wW", "b_w": "L0_conv_bW", "w_s": "L0_conv_wS", "b_s": "L0_conv_bS",
    "gamma": "L0_conv_gamma",
}


def build(nc, arrays):
    args = {}
    for short, a in arrays.items():
        args[short] = nc.dram_tensor(f"in_{short}", a.shape, mybir.dt.from_np(a.dtype), kind="ExternalInput").ap()
    out = nc.dram_tensor("out_0", arrays["x"].shape, F32, kind="ExternalOutput").ap()
    triple_gate_kernel(nc, **args, out=out)


def kernel(**inputs):
    import numpy as np
    import concourse.bacc as bacc
    from concourse.bass_utils import run_bass_kernel_spmd

    nc = bacc.Bacc("TRN2", target_bir_lowering=False, num_devices=1)
    arrays = {}
    for short, name in _INS.items():
        a = np.ascontiguousarray(inputs[name])
        arrays[short] = a.reshape(a.shape or (1,))
    build(nc, arrays)
    r = run_bass_kernel_spmd(nc, [{f"in_{k}": v for k, v in arrays.items()}], core_ids=[0])
    return r.results[0]["out_0"]
```

```python
from contextlib import ExitStack

import concourse.bass as bass
from concourse import mybir

F32 = mybir.dt.float32
BF16 = mybir.dt.bfloat16
ALU = mybir.AluOpType
ACT = mybir.ActivationFunctionType
AX = mybir.AxisListType

BN_EPS = 1e-5
TAPS = 7
PAD = TAPS // 2


def triple_gate_kernel(nc, x, bn_w, bn_b, w_h, b_h, w_w, b_w, w_s, b_s, gamma, out):
    N, C, H, W = x.shape
    P = 128
    HALVES = C // P
    ROWS = 8
    TILES = H // ROWS
    TOP = TILES // 2
    TPX = ROWS * W
    QROWS = 4
    QUADS = ROWS // QROWS
    QPX = QROWS * W
    PARTS = 3
    GROWS = 16
    GROUPS = H // GROWS
    GTILES = GROWS // ROWS
    SROW = PARTS * GROWS
    KROWS = SROW + PARTS
    CSUMS = 4
    LEAD = 13
    HALO = H // 2 + ROWS
    UP, LOW = 0, 1
    assert HALVES == QUADS == 2 and H == W == P and KROWS <= P

    BANDS = 3 * 2 * TAPS
    FLIPS = -(-BANDS // 4)
    CONSTS = 11 + 2 * PARTS
    VAR_STEPS, STAT_STEPS = 6, 17
    SPLIT = 2 * PARTS - 1

    TURN = {15 - LEAD + 1: LOW, 24 - LEAD + 1: UP}
    CONV = {}
    for turn_round, part in TURN.items():
        for n, taps in enumerate((range(0, 5), range(5, 10), range(10, 14))):
            CONV[turn_round + 1 + n // 2, n % 2] = (part, taps)
    SIGMOID = {r + 2: part for r, part in TURN.items()}
    POOLS = 6
    H_CONV = {(7 + n // 2, n % 2): range(3 * n, min(3 * n + 3, 14)) for n in range(5)}
    H_SIGMOID = 10

    with ExitStack() as ctx:
        def sb(name, shape, dt=F32):
            return ctx.enter_context(nc.sbuf_tensor(name, shape, dt))

        def pb(name, shape):
            return ctx.enter_context(nc.psum_tensor(name, shape, F32))

        def sem(name):
            return ctx.enter_context(nc.semaphore(name))

        image = sb("image", [P, TILES, HALVES, TPX])
        normed = sb("normed", [P, QUADS, HALVES, QPX])
        halfmax = sb("halfmax", [P, QUADS, QPX])
        scaled = sb("scaled", [P, HALVES, TPX])
        csum_row = sb("csum_row", [P, CSUMS, TPX // 4])
        bands = sb("bands", [P, 3, 2 * TAPS, P])
        pix = sb("pix", [P, 2, GROWS * W], BF16)
        gw_stack = sb("gw_stack", [P, GROUPS, C], BF16)
        z_h = sb("z_h", [P, 2, C + 2 * PAD])
        z_w = sb("z_w", [P, 2, C + 2 * PAD])
        z_s = sb("z_s", [P, 2, W + 2 * PAD])
        gates_h = sb("gates_h", [P, 2 * C])
        gate_h, gate_h_next = gates_h[:, 0:C], gates_h[:, C:2 * C]
        gate_ws = sb("gate_ws", [P, C + W])
        ws_parts = sb("ws_parts", [P, PARTS, C + W], BF16)
        pools = sb("pools", [P, 3, C])
        wmax = sb("wmax", [P, HALVES, H])
        cmax_t = sb("cmax_t", [P, H])
        ident = sb("ident", [P, P])
        mirror = sb("mirror", [P, P])
        zeros = sb("zeros", [P, C + W])
        mean_col = sb("mean_col", [P, 32])
        a_row = sb("a_row", [P, 4, P])
        a_row_w = sb("a_row_w", [P, C])
        taps_in = sb("taps_in", [P, TAPS])
        lines = sb("lines", [P, 2 * P])
        small = sb("small", [P, 64])
        totals = sb("totals", [P, N, HALVES])
        bands_flat = bands[:, :, :, :].rearrange("p g t q -> p (g t) q")
        folded = scaled[:, :, :].rearrange("p b (f r w) -> p b f r w", f=HALVES, w=W // 2)
        folded2 = halfmax[:, :, :].rearrange("p b (f r w) -> p b f r w", f=HALVES, w=W // 4)
        square_junk = normed[:, 0].rearrange("p f x -> p (f x)")
        hmax = normed[:, 1, :, 0:W]
        hmax_raw = normed[:, 1, :, W:2 * W]
        wsum = wmax
        squares = gates_h[:, 0:N * TILES * HALVES].rearrange("p (n t f) -> p n t f", t=TILES, f=HALVES)

        (SIGN, A, D, A3, D3, BNW, BNB, G3, BIAS, MEAN, VAR, RSTD, T0, T1, T2) = (4 * i for i in range(15))
        col = lambda n, f=0, k=1: small[:, n + f:n + f + k]

        gates_ps = pb("gates_ps", [P, HALVES, TPX])
        turn_ps = [pb("turn_ps0", [P, QPX]), pb("turn_ps1", [P, QPX])]
        csum_ps = pb("csum_ps", [P, QPX])
        conv_ps = pb("conv_ps", [P, QPX])

        kept = nc.dram_tensor("kept_pools", (N, P, 3, C), F32, kind="Internal").ap()
        via = nc.dram_tensor("via", (H, PARTS, C + W), BF16, kind="Internal").ap()
        via_w = via[:, :, 0:C].rearrange("(g r) a c -> a r g c", r=GROWS)
        via_s = via[:, :, C:].rearrange("(g r) a w -> g a r w", r=GROWS)
        via_lines = nc.dram_tensor("via_lines", (BANDS, 2 * P), F32, kind="Internal").ap()

        x_t = x.rearrange("n (f p) (t r) w -> n t p f (r w)", p=P, r=ROWS)
        out_t = out.rearrange("n (f p) (t r) w -> n t p f (r w)", p=P, r=ROWS)

        loaded = [sem(f"loaded{k}") for k in range(TILES)]
        stored = [sem(f"stored{k}") for k in range(TILES)]
        params = sem("params")
        tapped = sem("tapped")
        lined = sem("lined")
        lines_out = sem("lines_out")
        banded = sem("banded")
        band_turned = sem("band_turned")
        bands_ready = sem("bands_ready")
        consts = sem("consts")
        signed = sem("signed")
        squared = sem("squared")
        max_step = sem("max_step")
        fold_ready = sem("fold_ready")
        fold2_ready = sem("fold2_ready")
        fold_used = sem("fold_used")
        h_summed = sem("h_summed")
        h_maxed = sem("h_maxed")
        pools_ready = sem("pools_ready")
        pools_turned = sem("pools_turned")
        pools_out = sem("pools_out")
        pools_kept = sem("pools_kept")
        pools_in = sem("pools_in")
        stat = sem("stat")
        rooted = sem("rooted")
        rows_turned = sem("rows_turned")
        rows_out = sem("rows_out")
        z_scaled = sem("z_scaled")
        z_pooled = sem("z_pooled")
        normed_ready = sem("normed_ready")
        half_ready = sem("half_ready")
        turned = sem("turned")
        c_maxed = sem("c_maxed")
        c_summed = sem("c_summed")
        csum_out = sem("csum_out")
        csum_in = [sem(f"csum_in{b}") for b in range(CSUMS)]
        h_conv = sem("h_conv")
        h_sigmoid = sem("h_sigmoid")
        h_gate = sem("h_gate")
        pools_flat = sem("pools_flat")
        z_ready = sem("z_ready")
        ws_conv = sem("ws_conv")
        ws_gate = sem("ws_gate")
        ws_split = sem("ws_split")
        ws_left = sem("ws_left")
        w_stacked = sem("w_stacked")
        s_rows = [sem("s_rows0"), sem("s_rows1")]
        gates_ready = sem("gates_ready")
        scaled_ready = sem("scaled_ready")
        gated = sem("gated")
        added = sem("added")

        block = ctx.enter_context(nc.Block())

        def tile(n, k):
            return n * TILES + k

        def quad(m, k, q):
            return m * (TILES * QUADS) + (k * QUADS + q)

        unit = quad

        def pooled_tile(j, r):
            return (j, r + LEAD) if r + LEAD < TILES else (j + 1, r + LEAD - TILES)

        def gate_image(j, part):
            return j if part == LOW else j + 1

        def half_count(m, part):
            return 2 * m + part

        def quartered(k):
            return k % 4 != 3

        def quarters_before(k):
            return sum(quartered(i) for i in range(k))

        QUARTERED = quarters_before(TILES)

        OUT_ROWS = {UP: slice(0, H // 2), LOW: slice(H // 2, H)}
        OTHER = {UP: slice(H // 2, H), LOW: slice(0, H // 2)}
        IN_ROWS = {UP: slice(0, HALO), LOW: slice(0, H)}
        NEW_ROWS = {UP: slice(0, HALO), LOW: slice(H // 2, H)}
        NEW = {UP: HALO, LOW: H // 2}

        @block.sync
        def _(sp):
            with nc.allow_non_contiguous_dma(reason="294 taps, a line for each band matrix; parameters"):
                sp.dma_start(taps_in[0:2 * TAPS, :], w_h.rearrange("o i a b -> (o i a) b")).then_inc(tapped, 16)
                for g, src in ((1, w_w), (2, w_s)):
                    for i in range(2):
                        at = (g * 2 + i) * TAPS
                        sp.dma_start(taps_in[at:at + TAPS, :], src[0, i].rearrange("a b -> b a")
                                     ).then_inc(tapped, 16)
                for g, src in enumerate((b_h, b_w, b_s, gamma)):
                    at = BIAS + g if g < 3 else G3
                    sp.dma_start(small[:, at:at + 1], src.to_broadcast([P, 1])).then_inc(params, 16)
                sp.dma_start(col(BNW, 0, 2), bn_w.rearrange("(f p) -> p f", p=P)).then_inc(params, 16)
                sp.dma_start(col(BNB, 0, 2), bn_b.rearrange("(f p) -> p f", p=P)).then_inc(params, 16)

            for k in range(TILES):
                sp.dma_start(image[:, k], x_t[0, k]).then_inc(loaded[k], 16)
            sp.wait_ge(lined, 1 + TAPS)
            sp.dma_start(via_lines, lines[0:BANDS, :]).then_inc(lines_out, 16)
            sp.wait_ge(lines_out, 16)
            skewed = bass.AP(via_lines.tensor, 0, [[1, P], [2 * P, BANDS], [1, P]])
            sp.dma_start(bands_flat, skewed).then_inc(banded, 16)
            with sp.Fori(1, N) as n:
                for k in range(TILES):
                    halves_done = tile(n - 1, k + 1) * HALVES
                    sp.wait_ge(squared, halves_done)
                    sp.wait_ge(max_step, halves_done)
                    sp.wait_ge(fold_ready, halves_done)
                    sp.wait_ge(h_summed, halves_done)
                    sp.dma_start(image[:, k], x_t[n, k]).then_inc(loaded[k], 16)

            sp.wait_ge(pools_kept, 16 * N)
            sp.dma_start(pools[:, :, :], kept[N - 1]).then_inc(pools_in, 16)
            sp.wait_ge(consts, CONSTS)

            def place_gates(m, part):
                sp.wait_ge(ws_split, (half_count(m, part) + 1) * SPLIT)
                rows = OUT_ROWS[part]
                sp.dma_start(via[rows], ws_parts[rows, :, :]).then_inc(ws_left, 16)
                sp.wait_ge(ws_left, 16 * (half_count(m, part) + 1))
                groups = slice(part * GROUPS // 2, (part + 1) * GROUPS // 2)
                for a in range(PARTS):
                    sp.dma_start(gw_stack[a * GROWS:(a + 1) * GROWS, groups, :], via_w[a, :, groups, :]
                                 ).then_inc(w_stacked, 16)

            def spread_gate_s(g):
                rows = pix[SROW:KROWS, g % 2, :].rearrange("a (r w) -> a r w", w=W)
                sp.dma_start(rows, via_s[g]).then_inc(s_rows[g % 2], 16)

            def step(j, here, after, last=False):
                if not last:
                    sp.wait_ge(z_scaled, (j + 1) * 3)
                    sp.dma_start(pools[:, :, :], kept[after]).then_inc(pools_in, 16)
                for r in range(TILES):
                    if r == GTILES * (GROUPS // 2) - 1:
                        place_gates(j, LOW)
                    if r == TILES - 1 and not last:
                        place_gates(j + 1, UP)
                        spread_gate_s(0)
                    if r >= 1 and not last:
                        sp.wait_ge(stored[r - 1], 16 * (j + 1))
                        sp.dma_start(image[:, r - 1], x_t[after, r - 1]).then_inc(loaded[r - 1], 16)
                    sp.wait_ge(added, unit(j, r + 1, 0))
                    sp.dma_start(out_t[here, r], image[:, r]).then_inc(stored[r], 16)
                    done = (r + 1) // GTILES - 1
                    if r % GTILES == GTILES - 1:
                        if done in (2,):
                            pass
                        elif done == 3:
                            spread_gate_s(4)
                            spread_gate_s(5)
                        elif done + 2 < GROUPS:
                            spread_gate_s(done + 2)
                        elif done == GROUPS - 1 and not last:
                            spread_gate_s(1)
                if not last:
                    sp.wait_ge(stored[TILES - 1], 16 * (j + 1))
                    sp.dma_start(image[:, TILES - 1], x_t[after, TILES - 1]).then_inc(loaded[TILES - 1], 16)

            place_gates(0, UP)
            spread_gate_s(0)
            spread_gate_s(1)
            step(0, N - 1, 0)
            with sp.Fori(1, N - 1) as j:
                step(j, j - 1, j)
            step(N - 1, N - 2, None, last=True)
            for k in range(TILES):
                sp.wait_ge(stored[k], 16 * N)

        @block.gpsimd
        def _(pool):
            pool.memset(lines[:, :], 0.0).then_inc(lined, 1)
            pool.wait_ge(lined, 1)
            pool.wait_ge(tapped, 16 * 5)
            for k in range(TAPS):
                at = P - 1 - PAD + k
                pool.tensor_copy(lines[0:BANDS, at:at + 1], taps_in[0:BANDS, k:k + 1]
                                 ).then_inc(lined, 1)
            pool.memset(ident[:, :], 0.0).then_inc(consts, 1)
            pool.memset(mirror[:, :], 0.0).then_inc(consts, 1)
            pool.memset(mean_col[:, :], 1.0 / C).then_inc(consts, 1)
            pool.memset(zeros[:, :], 0.0).then_inc(consts, 1)
            for z in (z_h, z_w, z_s):
                pool.memset(z[:, :, :], 0.0).then_inc(consts, 1)
            pool.memset(pix[:, :, :], 0.0).then_inc(consts, 1)
            pool.memset(gw_stack[:, :, :], 1.0).then_inc(consts, 1)
            pool.wait_ge(consts, 9)
            pool.affine_select(out=ident[:, :], in_=ident[:, :], compare_op=ALU.not_equal, fill=1.0, base=0,
                               pattern=[[-1, P]], channel_multiplier=1).then_inc(consts, 1)
            pool.affine_select(out=mirror[:, :], in_=mirror[:, :], compare_op=ALU.not_equal, fill=1.0,
                               base=1 - P, pattern=[[1, P]], channel_multiplier=1).then_inc(consts, 1)

            def one_hots():
                for part in range(PARTS):
                    for b in range(2):
                        rows = pix[:, b, :].rearrange("p (r w) -> p r w", w=W)
                        pool.affine_select(out=rows, in_=rows, compare_op=ALU.not_equal, fill=1.0,
                                           base=-part * GROWS, pattern=[[-1, GROWS], [0, W]],
                                           channel_multiplier=1).then_inc(consts, 1)
                    pool.wait_ge(consts, 11 + 2 * (part + 1))

            def sweep1(n, first=False):
                for k in range(TILES):
                    b = k % 2
                    pool.wait_ge(loaded[k], 16 * (n + 1))
                    if not (first and k < 2):
                        pool.wait_ge(fold_used, tile(n, k) - 1)
                    px = image[:, k].rearrange("p f (r w) -> p f r w", w=W)
                    pool.tensor_tensor(folded[:, b], px[:, :, :, 0:W // 2], px[:, :, :, W // 2:W],
                                       ALU.add).then_inc(fold_ready, 2)
                    if quartered(k):
                        pool.wait_ge(fold_ready, tile(n, k + 1) * 2)
                        pool.tensor_tensor(folded2[:, b], folded[:, b, :, :, 0:W // 4],
                                           folded[:, b, :, :, W // 4:W // 2], ALU.add).then_inc(fold2_ready, 1)

            sweep1(0, True)
            one_hots()
            with pool.Fori(1, N) as n:
                sweep1(n)

            def normalise_pools(m):
                a_all = a_row[:, 0:2, :].rearrange("p a q -> p (a q)")
                d_all = a_row[:, 2:4, :].rearrange("p a q -> p (a q)")
                places = (z_h[:, 1, PAD:PAD + C], z_h[:, 0, PAD:PAD + C], z_w[:, 1, PAD:PAD + C])
                pool.wait_ge(pools_in, 16 * (m + 1))
                for n, scale in enumerate((a_row_w[:, :], a_all, a_row_w[:, :])):
                    pool.tensor_tensor(places[n], pools[:, n, :], scale, ALU.mult).then_inc(z_scaled, 1)
                pool.wait_ge(z_scaled, 3 * (m + 1))
                for z in places:
                    last = pool.tensor_tensor(z, z, d_all, ALU.add)
                last.then_inc(z_pooled, 1)

            def split(m, part, before=None, first=False):
                rows = OUT_ROWS[part]
                value = gate_ws[rows, :]
                n = half_count(m, part)
                if before is not None:
                    pool.wait_ge(added, before)
                pool.wait_ge(ws_gate, 2 * (n + 1))
                if not first:
                    pool.wait_ge(ws_left, 16 * n)
                for a in range(PARTS):
                    pool.tensor_tensor(ws_parts[rows, a, :], value, zeros[rows, :], ALU.add
                                       ).then_inc(ws_split, 1)
                    if a + 1 < PARTS:
                        pool.wait_ge(ws_split, SPLIT * n + 2 * a + 1)
                        pool.tensor_tensor(value, value, ws_parts[rows, a, :], ALU.subtract
                                           ).then_inc(ws_split, 1)
                    pool.wait_ge(ws_split, SPLIT * n + min(2 * a + 2, SPLIT))

            def add_x(j, r, f):
                pool.wait_ge(gated, unit(j, r, f) + 1)
                pool.tensor_tensor(image[:, r, f, :], image[:, r, f, :], scaled[:, f, :], ALU.add
                                   ).then_inc(added, 1)

            def rounds(j, last=False):
                for r in range(TILES):
                    for f in range(HALVES):
                        add_x(j, r, f)
                    if r == POOLS and not last:
                        pool.wait_ge(ws_conv, half_count(j, LOW) + 1)
                        normalise_pools(j + 1)
                    if r in SIGMOID and not (last and SIGMOID[r] == UP):
                        split(gate_image(j, SIGMOID[r]), SIGMOID[r], before=unit(j, r + 1, 0))

            pool.wait_ge(rows_out, 2)
            normalise_pools(0)
            split(0, UP, first=True)
            with pool.Fori(0, N - 1) as j:
                rounds(j)
            rounds(N - 1, last=True)

        @block.scalar
        def _(act):
            def sweep1(n, first=False):
                for k in range(TILES):
                    act.wait_ge(loaded[k], 16 * (n + 1))
                    for f in range(HALVES):
                        if not (first and k == 0 and f == 0):
                            act.wait_ge(squared, tile(n, k) * HALVES + f)
                        act.activation(square_junk, image[:, k, f, :], ACT.Square,
                                       accum_out=squares[:, n, k, f:f + 1]).then_inc(squared, 1)
                act.wait_ge(pools_turned, n + 1)
                if not first:
                    act.wait_ge(pools_kept, 16 * n)
                act.activation(pools[:, 0, :], conv_ps[:, 0:C], ACT.Identity)
                act.activation(pools[:, 1:3, :].rearrange("p a c -> p (a c)"), csum_ps[:, :],
                               ACT.Identity).then_inc(pools_out, 1)
                act.wait_ge(pools_out, n + 1)
                act.dma_start(kept[n], pools[:, :, :]).then_inc(pools_kept, 16)

            sweep1(0, True)
            for n in range(FLIPS):
                act.wait_ge(band_turned, n + 1)
                four = bands_flat[:, 4 * n:min(4 * n + 4, BANDS)].rearrange("p b q -> p (b q)")
                act.activation(four, turn_ps[n % 2][:, 0:four.shape[1]], ACT.Identity).then_inc(bands_ready, 1)
            with act.Fori(1, N) as n:
                sweep1(n)
            act.wait_ge(stat, VAR_STEPS)
            act.activation(col(RSTD, 0, 2), col(VAR, 0, 2), ACT.Sqrt).then_inc(rooted, 1)
            act.wait_ge(stat, STAT_STEPS)

            def normalise(m, k, q, first=False):
                if q == 0:
                    act.wait_ge(loaded[k], 16 * (N + m))
                if not (first and k == 0):
                    act.wait_ge(half_ready, quad(m, k, q) - 1)
                    act.wait_ge(c_summed, tile(m, k))
                for f in range(HALVES):
                    last = act.activation(normed[:, q, f, :], image[:, k, f, q * QPX:(q + 1) * QPX],
                                          ACT.Identity, scale=col(A, f), bias=col(D, f))
                last.then_inc(normed_ready, 1)

            def csum_leaves(m, k, first=False):
                act.wait_ge(c_summed, tile(m, k + 1))
                b = k % CSUMS
                if not (first and k < CSUMS):
                    act.wait_ge(csum_in[b], 32 * (m * (TILES // CSUMS) + k // CSUMS))
                act.activation(csum_row[:, b, :], csum_ps[:, 0:TPX // 4], ACT.Identity).then_inc(csum_out, 1)
                if k < CSUMS - 2:
                    return
                act.wait_ge(csum_out, tile(m, k + 1))
                if k == CSUMS - 2 and not first:
                    act.wait_ge(ws_conv, half_count(m, UP))
                for kk in range(0 if k == CSUMS - 2 else k, k + 1):
                    for i in range(2):
                        h0 = kk * ROWS
                        act.dma_start(z_s[h0 + i:h0 + ROWS:2, 1, PAD:PAD + W],
                                      csum_row[0:P:32, kk % CSUMS, i * W:(i + 1) * W]
                                      ).then_inc(csum_in[kk % CSUMS], 16)

            def scale(j, r, f, first=False):
                if not (first and r == 0):
                    act.wait_ge(added, unit(j, r, f) - 1)
                act.activation(scaled[:, f, :], image[:, r, f, :], ACT.Identity,
                               scale=col(A3, f), bias=col(D3, f)).then_inc(scaled_ready, 1)

            def sigmoid_h(m, first=False):
                act.wait_ge(h_conv, m + 1)
                if not first:
                    act.wait_ge(h_gate, m)
                act.activation(gate_h_next, conv_ps[:, 0:C], ACT.Sigmoid, bias=col(BIAS, 0)
                               ).then_inc(h_sigmoid, 1)

            def pass_gate_h(m, first=False):
                act.wait_ge(h_sigmoid, m + 1)
                if not first:
                    act.wait_ge(gates_ready, unit(m, 0, 0))
                act.activation(gate_h, gate_h_next, ACT.Identity).then_inc(h_gate, 1)

            def sigmoids(m, part, first=False):
                n = half_count(m, part)
                act.wait_ge(ws_conv, n + 1)
                if not first:
                    act.wait_ge(ws_split, SPLIT * n)
                rows, other = OUT_ROWS[part], OTHER[part]
                act.activation(gate_ws[rows, 0:C], conv_ps[rows, 0:C], ACT.Sigmoid,
                               bias=small[rows, BIAS + 1:BIAS + 2]).then_inc(ws_gate, 1)
                act.activation(gate_ws[rows, C:C + W], conv_ps[other, C:C + W], ACT.Sigmoid,
                               bias=small[other, BIAS + 2:BIAS + 3]).then_inc(ws_gate, 1)

            for k in range(LEAD):
                for q in range(QUADS):
                    normalise(0, k, q, True)
                csum_leaves(0, k, True)
            sigmoid_h(0, True)
            pass_gate_h(0, True)
            sigmoids(0, UP, True)

            def rounds(j, first=False, last=False):
                for r in range(TILES):
                    m, k = pooled_tile(j, r)
                    pooling = not (last and r + LEAD >= TILES)
                    for n in range(2):
                        scale(j, r, n, first)
                        if pooling:
                            normalise(m, k, n)
                    if pooling:
                        csum_leaves(m, k)
                    if r == H_SIGMOID and not last:
                        sigmoid_h(j + 1)
                    if r in SIGMOID and not (last and SIGMOID[r] == UP):
                        sigmoids(gate_image(j, SIGMOID[r]), SIGMOID[r])
                if not last:
                    pass_gate_h(j + 1)

            rounds(0, first=True)
            with act.Fori(1, N - 1) as j:
                rounds(j)
            rounds(N - 1, last=True)

        @block.vector
        def _(dve):
            dve.wait_ge(params, 16 * 6)
            dve.tensor_scalar(col(T0, 0, 2), col(BNW, 0, 2), 0.0, None, ALU.is_ge).then_inc(signed, 1)
            dve.wait_ge(signed, 1)
            dve.tensor_scalar(col(SIGN, 0, 2), col(T0, 0, 2), 2.0, -1.0, ALU.mult, ALU.add).then_inc(signed, 1)
            dve.wait_ge(signed, 2)

            def sweep1(n, first=False):
                for k in range(TILES):
                    dve.wait_ge(loaded[k], 16 * (n + 1))
                    for f in range(HALVES):
                        if k == 0:
                            if not first:
                                dve.wait_ge(h_maxed, 2 * n)
                            op = dve.tensor_scalar(gates_ps[:, f, :], image[:, k, f, :], col(SIGN, f), None,
                                                   ALU.mult)
                        else:
                            dve.wait_ge(max_step, tile(n, k) * HALVES + f - 1)
                            op = dve.scalar_tensor_tensor(
                                out=gates_ps[:, f, :], in0=image[:, k, f, :], scalar=col(SIGN, f),
                                in1=gates_ps[:, f, :], op0=ALU.mult, op1=ALU.max)
                        op.then_inc(max_step, 1)
                    if not first and k == 0:
                        dve.wait_ge(pools_turned, n)
                    if quartered(k):
                        dve.wait_ge(fold2_ready, n * QUARTERED + quarters_before(k) + 1)
                        sums = folded2[:, k % 2]
                    else:
                        dve.wait_ge(fold_ready, tile(n, k + 1) * 2)
                        sums = folded[:, k % 2]
                    dve.tensor_reduce(wsum[:, :, k * ROWS:(k + 1) * ROWS], sums, AX.X, ALU.add
                                      ).then_inc(fold_used, 1)
                dve.wait_ge(max_step, tile(n, TILES) * HALVES)
                for f in range(HALVES):
                    last = dve.tensor_reduce(hmax_raw[:, f], gates_ps[:, f, :].rearrange(
                        "p (r w) -> p w r", w=W), AX.X, ALU.max)
                last.then_inc(h_maxed, 1)
                dve.wait_ge(fold_used, tile(n, TILES))
                dve.tensor_reduce(totals[:, n, :], wsum[:, :, :], AX.X, ALU.add).then_inc(h_maxed, 1)
                dve.wait_ge(h_maxed, 2 * n + 2)
                for f in range(HALVES):
                    last = dve.tensor_scalar(hmax[:, f], hmax_raw[:, f], col(SIGN, f), None, ALU.mult)
                last.then_inc(pools_ready, 1)

            sweep1(0, True)
            with dve.Fori(1, N) as n:
                sweep1(n)

            dve.wait_ge(squared, N * TILES * HALVES)
            dve.wait_ge(pools_turned, N)
            done = [0]

            def chain(op):
                done[0] += 1
                op.then_inc(stat, 1)
                dve.wait_ge(stat, done[0])

            two = lambda c: col(c, 0, 2)
            count = N * H * W
            chain(dve.tensor_reduce(two(MEAN), totals[:, :, :].rearrange("p n f -> p f n"), AX.X, ALU.add))
            chain(dve.tensor_reduce(two(VAR), squares[:, :, :, :].rearrange("p n t f -> p f (n t)"), AX.X,
                                    ALU.add))
            chain(dve.tensor_scalar(two(MEAN), two(MEAN), 1.0 / count, None, ALU.mult))
            chain(dve.tensor_tensor(two(T0), two(MEAN), two(MEAN), ALU.mult))
            chain(dve.tensor_scalar(two(VAR), two(VAR), 1.0 / count, BN_EPS, ALU.mult, ALU.add))
            chain(dve.tensor_tensor(two(VAR), two(VAR), two(T0), ALU.subtract))
            assert done[0] == VAR_STEPS
            dve.wait_ge(rooted, 1)
            chain(dve.reciprocal(two(T1), two(RSTD)))
            chain(dve.tensor_tensor(two(T2), two(T1), two(T1), ALU.mult))
            chain(dve.tensor_tensor(two(T2), two(T2), two(VAR), ALU.mult))
            chain(dve.tensor_scalar(two(T2), two(T2), -0.5, 1.5, ALU.mult, ALU.add))
            chain(dve.tensor_tensor(two(T1), two(T1), two(T2), ALU.mult))
            chain(dve.tensor_tensor(two(A), two(BNW), two(T1), ALU.mult))
            chain(dve.tensor_tensor(two(T0), two(MEAN), two(A), ALU.mult))
            chain(dve.tensor_tensor(two(D), two(BNB), two(T0), ALU.subtract))
            chain(dve.tensor_scalar(col(G3), col(G3), 1.0 / 3.0, None, ALU.mult))
            chain(dve.tensor_scalar(two(A3), two(A), col(G3), None, ALU.mult))
            chain(dve.tensor_scalar(two(D3), two(D), col(G3), None, ALU.mult))
            assert done[0] == STAT_STEPS
            dve.wait_ge(rows_turned, 1)
            dve.tensor_copy(a_row[:, :, :].rearrange("p a q -> p (a q)"), turn_ps[0][:, :]).then_inc(rows_out, 1)
            dve.tensor_scalar(a_row_w[:, :], turn_ps[0][:, 0:C], 1.0 / W, None, ALU.mult).then_inc(rows_out, 1)

            def pool_quad(m, k, q, first=False):
                dve.wait_ge(normed_ready, quad(m, k, q) + 1)
                if not first and q == 0 and k in (0, TOP):
                    dve.wait_ge(pools_flat, half_count(m, UP) - 1 + k // TOP)
                h0 = k * ROWS + q * QROWS
                dve.tensor_reduce(wmax[:, :, h0:h0 + QROWS],
                                  normed[:, q].rearrange("p f (r w) -> p f r w", w=W), AX.X, ALU.max)
                if not (first and k == 0):
                    dve.wait_ge(turned, quad(m, k, q) - 1)
                dve.tensor_tensor(halfmax[:, q, :], normed[:, q, 0, :], normed[:, q, 1, :],
                                  ALU.max).then_inc(half_ready, 1)

            def cmax_quad(m, k, q):
                dve.wait_ge(turned, quad(m, k, q) + 1)
                h0 = k * ROWS + q * QROWS
                dve.tensor_reduce(cmax_t[:, h0:h0 + QROWS],
                                  turn_ps[q][:, :].rearrange("p (r c) -> p r c", c=P), AX.X, ALU.max
                                  ).then_inc(c_maxed, 1)

            def gate_unit(j, r, f):
                dve.wait_ge(gates_ready, unit(j, r, f) + 1)
                dve.wait_ge(scaled_ready, unit(j, r, f) + 1)
                dve.tensor_tensor(scaled[:, f, :], gates_ps[:, f, :], scaled[:, f, :], ALU.mult
                                  ).then_inc(gated, 1)

            def take_pools(m, part, first=False):
                dve.wait_ge(pools_flat, half_count(m, part) + 1)
                if not first:
                    dve.wait_ge(ws_conv, half_count(m, part))
                rows, new = NEW_ROWS[part], NEW[part]
                dve.tensor_copy(z_w[rows, 0, PAD:PAD + C], conv_ps[0:new, 0:C]).then_inc(z_ready, 1)
                dve.tensor_copy(z_s[rows, 0, PAD:PAD + W], conv_ps[0:new, C:C + W]).then_inc(z_ready, 1)

            for k in range(LEAD):
                for q in range(QUADS):
                    pool_quad(0, k, q, True)
                    cmax_quad(0, k, q)
            take_pools(0, UP, True)

            def rounds(j, last=False):
                for r in range(TILES):
                    m, k = pooled_tile(j, r)
                    pooling = not (last and r + LEAD >= TILES)
                    for n in range(2):
                        if pooling:
                            pool_quad(m, k, n)
                        gate_unit(j, r, n)
                        if pooling:
                            cmax_quad(m, k, n)
                    if r in TURN and not (last and TURN[r] == UP):
                        take_pools(gate_image(j, TURN[r]), TURN[r])

            with dve.Fori(0, N - 1) as j:
                rounds(j)
            rounds(N - 1, last=True)

        @block.tensor
        def _(pe):
            pe.wait_ge(consts, 11)

            def turn(dst, src, start=True, stop=True):
                return pe.matmul(dst, src, ident[:, :], start=start, stop=stop, is_transpose=True,
                                 skip_group_check=True)

            def sweep1(n, first=False):
                for k in range(TILES):
                    pe.wait_ge(loaded[k], 16 * (n + 1))
                    if not first and k == 0:
                        pe.wait_ge(pools_out, n)
                    for f in range(HALVES):
                        for r in range(ROWS):
                            last = turn(conv_ps[:, f * P:(f + 1) * P], image[:, k, f, r * W:(r + 1) * W],
                                        start=(k == 0 and f == 0 and r == 0),
                                        stop=(k == TILES - 1 and r == ROWS - 1))
                        last.then_inc(h_summed, 1)
                pe.wait_ge(pools_ready, n + 1)
                for f in range(HALVES):
                    turn(csum_ps[:, f * P:(f + 1) * P], hmax[:, f])
                for f in range(HALVES):
                    last = turn(csum_ps[:, C + f * P:C + (f + 1) * P], wsum[:, f])
                last.then_inc(pools_turned, 1)

            sweep1(0, True)
            pe.wait_ge(banded, 16)
            for n in range(FLIPS):
                if n >= 2:
                    pe.wait_ge(bands_ready, n - 1)
                for i, band in enumerate(range(4 * n, min(4 * n + 4, BANDS))):
                    last = pe.matmul(turn_ps[n % 2][:, i * P:(i + 1) * P], bands_flat[:, band], mirror[:, :],
                                     start=True, stop=True, is_transpose=True, skip_group_check=True)
                last.then_inc(band_turned, 1)
            with pe.Fori(1, N) as n:
                sweep1(n)

            pe.wait_ge(stat, STAT_STEPS)
            for i, c in enumerate((A, A + 1, D, D + 1)):
                last = pe.matmul(turn_ps[0][:, i * P:(i + 1) * P], small[:, c:c + 1].to_broadcast([P, P]),
                                 ident[:, :], start=True, stop=True)
            last.then_inc(rows_turned, 1)
            pe.wait_ge(rows_out, 2)
            pe.wait_ge(bands_ready, FLIPS)

            def turn_quad(m, k, q, first=False):
                pe.wait_ge(half_ready, quad(m, k, q) + 1)
                if not (first and k == 0):
                    pe.wait_ge(c_maxed, quad(m, k, q) - 1)
                for r in range(QROWS):
                    last = turn(turn_ps[q][:, r * P:(r + 1) * P], halfmax[:, q, r * W:(r + 1) * W])
                last.then_inc(turned, 1)

            def csum_tile(m, k, first=False):
                pe.wait_ge(normed_ready, quad(m, k + 1, 0))
                if not (first and k == 0):
                    pe.wait_ge(csum_out, tile(m, k))
                for f in range(HALVES):
                    for two_rows in range(ROWS // 2):
                        q, at = two_rows // 2, (two_rows % 2) * 2 * W
                        group = slice(32 * two_rows, 32 * (two_rows + 1))
                        last = pe.matmul(csum_ps[group, 0:2 * W], mean_col[:, :], normed[:, q, f, at:at + 2 * W],
                                         start=(f == 0), stop=(f == HALVES - 1), tile_position=(0, group.start))
                last.then_inc(c_summed, 1)

            def convolve(rows_in, rows_out, rows_to, at, g, z, width, tap):
                i, o = divmod(tap, TAPS)
                return pe.matmul(conv_ps[rows_to, at:at + width], bands[rows_in, g, tap, rows_out],
                                 z[rows_in, i, o:o + width], start=(tap == 0), stop=(tap == 2 * TAPS - 1))

            def conv_h(m, taps, first=False):
                if taps[0] == 0:
                    pe.wait_ge(z_pooled, m + 1)
                    if not first:
                        pe.wait_ge(ws_gate, 2 * half_count(m, UP))
                for tap in taps:
                    last = convolve(slice(0, P), slice(0, P), slice(0, P), 0, 0, z_h, C, tap)
                if taps[-1] == 2 * TAPS - 1:
                    last.then_inc(h_conv, 1)

            def await_pools(m, part):
                if part == UP:
                    pe.wait_ge(h_sigmoid, m + 1)
                else:
                    pe.wait_ge(ws_gate, 2 * half_count(m, part))
                seen = quad(m, TOP + 1 if part == UP else TILES, 0)
                pe.wait_ge(half_ready, seen)
                pe.wait_ge(c_maxed, seen)

            def flatten_pools(part):
                rows, new = NEW_ROWS[part], NEW[part]
                for f in range(HALVES):
                    turn(conv_ps[0:new, f * P:(f + 1) * P], wmax[:, f, rows])
                turn(conv_ps[0:new, C:C + W], cmax_t[:, rows]).then_inc(pools_flat, 1)

            def conv_ws(m, part, taps):
                if taps[0] == 0:
                    pe.wait_ge(z_pooled, m + 1)
                    pe.wait_ge(z_ready, 2 * (half_count(m, part) + 1))
                    rows_tiles = TOP + 1 if part == UP else TILES
                    for b in range(CSUMS):
                        uses = (rows_tiles - b + CSUMS - 1) // CSUMS
                        pe.wait_ge(csum_in[b], 32 * (m * (TILES // CSUMS) + uses))
                for tap in taps:
                    convolve(IN_ROWS[part], OUT_ROWS[part], OUT_ROWS[part], 0, 1, z_w, C, tap)
                    last = convolve(IN_ROWS[part], OUT_ROWS[part], OTHER[part], C, 2, z_s, W, tap)
                if taps[-1] == 2 * TAPS - 1:
                    last.then_inc(ws_conv, 1)

            def spread(j, r, f, first=False):
                g = r // GTILES
                if r == 0 and f == 0:
                    pe.wait_ge(h_gate, j + 1)
                if r in (0, TOP) and f == 0:
                    pe.wait_ge(w_stacked, 16 * PARTS * (half_count(j, r // TOP) + 1))
                if r % GTILES == 0 and f == 0:
                    pe.wait_ge(s_rows[g % 2], 16 * (j * (GROUPS // 2) + g // 2 + 1))
                if not (first and r == 0):
                    pe.wait_ge(gated, unit(j, r, f) - 1)
                for q in range(QUADS):
                    px = (r % GTILES) * TPX + q * QPX
                    dst = gates_ps[:, f, q * QPX:(q + 1) * QPX]
                    pe.matmul(dst, gw_stack[0:KROWS, g, f * P:(f + 1) * P], pix[0:KROWS, g % 2, px:px + QPX],
                              start=True, stop=False, skip_group_check=True)
                    for row in range(QROWS):
                        last = turn(dst[:, row * W:(row + 1) * W], gate_h[:, f * P:(f + 1) * P], start=False,
                                    stop=(row == QROWS - 1))
                last.then_inc(gates_ready, 1)

            for k in range(LEAD):
                turn_quad(0, k, 0, True)
                csum_tile(0, k, True)
                turn_quad(0, k, 1, True)
            conv_h(0, range(2 * TAPS), True)
            await_pools(0, UP)
            flatten_pools(UP)
            conv_ws(0, UP, range(2 * TAPS))
            pe.wait_ge(consts, CONSTS)

            def rounds(j, first=False, last=False):
                for r in range(TILES):
                    m, k = pooled_tile(j, r)
                    pooling = not (last and r + LEAD >= TILES)
                    for n in range(2):
                        spread(j, r, n, first)
                        turning = n == 0 and r in TURN and not (last and TURN[r] == UP)
                        if turning:
                            await_pools(gate_image(j, TURN[r]), TURN[r])
                        if pooling:
                            if n == 1:
                                csum_tile(m, k)
                            turn_quad(m, k, n)
                        if turning:
                            flatten_pools(TURN[r])
                        if (r, n) in CONV and not (last and CONV[r, n][0] == UP):
                            part, taps = CONV[r, n]
                            conv_ws(gate_image(j, part), part, taps)
                        if (r, n) in H_CONV and not last:
                            conv_h(j + 1, H_CONV[r, n])

            rounds(0, first=True)
            with pe.Fori(1, N - 1) as j:
                rounds(j)
            rounds(N - 1, last=True)


_INS = {
    "x": "x", "bn_w": "L0_conv_bn_w", "bn_b": "L0_conv_bn_b", "w_h": "L0_conv_wH", "b_h": "L0_conv_bH",
    "w_w": "L0_conv_wW", "b_w": "L0_conv_bW", "w_s": "L0_conv_wS", "b_s": "L0_conv_bS",
    "gamma": "L0_conv_gamma",
}


def build(nc, arrays):
    args = {}
    for short, a in arrays.items():
        args[short] = nc.dram_tensor(f"in_{short}", a.shape, mybir.dt.from_np(a.dtype), kind="ExternalInput").ap()
    out = nc.dram_tensor("out_0", arrays["x"].shape, F32, kind="ExternalOutput").ap()
    triple_gate_kernel(nc, **args, out=out)


def kernel(**inputs):
    import numpy as np
    import concourse.bacc as bacc
    from concourse.bass_utils import run_bass_kernel_spmd

    nc = bacc.Bacc("TRN2", target_bir_lowering=False, num_devices=1)
    arrays = {}
    for short, name in _INS.items():
        a = np.ascontiguousarray(inputs[name])
        arrays[short] = a.reshape(a.shape or (1,))
    build(nc, arrays)
    r = run_bass_kernel_spmd(nc, [{f"in_{k}": v for k, v in arrays.items()}], core_ids=[0])
    return r.results[0]["out_0"]
```

```python
from contextlib import ExitStack

import concourse.bass as bass
from concourse import mybir

F32 = mybir.dt.float32
BF16 = mybir.dt.bfloat16
ALU = mybir.AluOpType
ACT = mybir.ActivationFunctionType
AX = mybir.AxisListType

BN_EPS = 1e-5
TAPS = 7
PAD = TAPS // 2


def triple_gate_kernel(nc, x, bn_w, bn_b, w_h, b_h, w_w, b_w, w_s, b_s, gamma, out):
    N, C, H, W = x.shape
    P = 128
    HALVES = C // P
    ROWS = 8
    TILES = H // ROWS
    TOP = TILES // 2
    TPX = ROWS * W
    QROWS = 4
    QUADS = ROWS // QROWS
    QPX = QROWS * W
    PARTS = 3
    GROWS = 16
    GROUPS = H // GROWS
    GTILES = GROWS // ROWS
    SROW = PARTS * GROWS
    KROWS = SROW + PARTS
    COLS = P // QROWS
    LEAD = 12
    HALO = H // 2 + QROWS
    UP, LOW = 0, 1
    assert HALVES == QUADS == 2 and H == W == P and KROWS <= P and COLS == TILES * QUADS
    assert N * TILES * HALVES <= 2 * C

    BANDS = 3 * 2 * TAPS
    FLIPS = -(-BANDS // 4)
    IDENTS = 12
    CONSTS = IDENTS + 2 + 2 * PARTS
    VAR_STEPS, STAT_STEPS = 7, 18
    SPLIT = 2 * PARTS - 1

    TURN = {2 * (TILES - LEAD): LOW, 2 * (TILES + TOP - LEAD) + 1: UP}
    CSUM_OUT = {2 * (TILES - LEAD): LOW, 2 * (TILES + TOP - LEAD) + 2: UP}
    CONV = {}
    for turn_step, part in TURN.items():
        for n, taps in enumerate((range(0, TAPS), range(TAPS, 2 * TAPS))):
            CONV[turn_step + 1 + n] = (part, taps)
    SIGMOID = {step + 1: part for step, (part, taps) in CONV.items() if taps[-1] == 2 * TAPS - 1}
    PLACE = {(step - 1) // 2: part for step, part in SIGMOID.items()}
    S_ROWS = {(GTILES * (g - 1) - 1) % TILES: g for g in range(GROUPS) if g % (GROUPS // 2)}
    POOLS = range(13, 16)
    H_CONV = {17 + n: range(3 * n, min(3 * n + 3, 2 * TAPS)) for n in range(5)}
    H_SIGMOID = max(H_CONV) + 1
    TAIL = 2 * (TILES - LEAD) + 4
    DVE_ADDS = range(TAIL, 2 * TILES, 3)
    assert TAIL % 4 == 0

    with ExitStack() as ctx:
        def sb(name, shape, dt=F32):
            return ctx.enter_context(nc.sbuf_tensor(name, shape, dt))

        def pb(name, shape):
            return ctx.enter_context(nc.psum_tensor(name, shape, F32))

        def sem(name):
            return ctx.enter_context(nc.semaphore(name))

        image = sb("image", [P, TILES, HALVES, TPX])
        normed = sb("normed", [P, QUADS, HALVES, QPX])
        halfmax = sb("halfmax", [P, QUADS, QPX])
        scaled = sb("scaled", [P, HALVES, TPX])
        bands = sb("bands", [P, 3, 2 * TAPS, P])
        pix = sb("pix", [P, 2, GROWS * W], BF16)
        gw_stack = sb("gw_stack", [P, GROUPS, C], BF16)
        z_h = sb("z_h", [P, 2, C + 2 * PAD])
        z_w = sb("z_w", [P, 2, C + 2 * PAD])
        z_s = sb("z_s", [P, 2, W + 2 * PAD])
        gates_h = sb("gates_h", [P, 2 * C])
        gate_h, gate_h_next = gates_h[:, 0:C], gates_h[:, C:2 * C]
        gate_ws = sb("gate_ws", [P, (C + W) // 2])
        ws_parts = sb("ws_parts", [P, PARTS, (C + W) // 2], BF16)
        pools = sb("pools", [P, 3, C])
        wmax = sb("wmax", [P, HALVES, H])
        cmax_t = sb("cmax_t", [P, QROWS, COLS])
        ident = sb("ident", [P, P])
        mirror = sb("mirror", [P, P])
        zeros = sb("zeros", [P, (C + W) // 2])
        mean_strip = sb("mean_strip", [P, 2 * COLS])
        a_row = sb("a_row", [P, 4, P])
        a_row_w = sb("a_row_w", [P, C])
        taps_in = sb("taps_in", [P, TAPS])
        lines = sb("lines", [P, 2 * P])
        small = sb("small", [P, 64])
        totals = sb("totals", [P, N, HALVES])
        bands_flat = bands[:, :, :, :].rearrange("p g t q -> p (g t) q")
        folded = scaled[:, :, :].rearrange("p b (f r w) -> p b f r w", f=HALVES, w=W // 2)
        folded2 = halfmax[:, :, :].rearrange("p b (f r w) -> p b f r w", f=HALVES, w=W // 4)
        square_junk = normed[:, 0].rearrange("p f x -> p (f x)")
        hmax = normed[:, 1, :, 0:W]
        hmax_raw = normed[:, 1, :, W:2 * W]
        wsum = wmax
        squares = gates_h[:, 0:N * TILES * HALVES].rearrange("p (n t f) -> p n t f", t=TILES, f=HALVES)

        (SIGN, A, D, A3, D3, BNW, BNB, G3, BIAS, MEAN, VAR, RSTD, T0, T1, T2, SHIFT) = (4 * i for i in range(16))
        col = lambda n, f=0, k=1: small[:, n + f:n + f + k]

        gates_ps = pb("gates_ps", [P, HALVES, TPX])
        turn_ps = [pb("turn_ps0", [P, QPX]), pb("turn_ps1", [P, QPX])]
        csum_ps = pb("csum_ps", [P, QPX])
        conv_ps = pb("conv_ps", [P, QPX])

        kept = nc.dram_tensor("kept_pools", (N, P, 3, C), F32, kind="Internal").ap()
        via_w = nc.dram_tensor("via_w", (H, PARTS, C), BF16, kind="Internal").ap()
        via_s = nc.dram_tensor("via_s", (H, PARTS, W), BF16, kind="Internal").ap()
        via_lines = nc.dram_tensor("via_lines", (BANDS, 2 * P), F32, kind="Internal").ap()

        x_t = x.rearrange("n (f p) (t r) w -> n t p f (r w)", p=P, r=ROWS)
        out_t = out.rearrange("n (f p) (t r) w -> n t p f (r w)", p=P, r=ROWS)

        loaded = [sem(f"loaded{k}") for k in range(TILES)]
        stored = [sem(f"stored{k}") for k in range(TILES)]
        weights = sem("weights")
        params = sem("params")
        tapped = sem("tapped")
        lined = sem("lined")
        lines_out = sem("lines_out")
        banded = sem("banded")
        band_turned = sem("band_turned")
        bands_ready = sem("bands_ready")
        consts = sem("consts")
        signed = sem("signed")
        shifted = sem("shifted")
        squared = sem("squared")
        max_step = sem("max_step")
        fold_ready = sem("fold_ready")
        fold2_ready = sem("fold2_ready")
        fold_used = sem("fold_used")
        h_summed = sem("h_summed")
        h_maxed = sem("h_maxed")
        pools_ready = sem("pools_ready")
        pools_turned = sem("pools_turned")
        pools_out = sem("pools_out")
        pools_kept = sem("pools_kept")
        pools_in = sem("pools_in")
        stat = sem("stat")
        rooted = sem("rooted")
        rows_turned = sem("rows_turned")
        rows_out = sem("rows_out")
        z_scaled = sem("z_scaled")
        z_pooled = sem("z_pooled")
        normed_ready = sem("normed_ready")
        half_ready = sem("half_ready")
        turned = sem("turned")
        c_maxed = sem("c_maxed")
        c_summed = sem("c_summed")
        csum_out = sem("csum_out")
        h_conv = sem("h_conv")
        h_sigmoid = sem("h_sigmoid")
        h_gate = sem("h_gate")
        pools_flat = sem("pools_flat")
        z_ready = sem("z_ready")
        ws_conv = sem("ws_conv")
        ws_gate = sem("ws_gate")
        ws_split = sem("ws_split")
        w_left = sem("w_left")
        s_left = sem("s_left")
        w_stacked = sem("w_stacked")
        s_rows = [sem("s_rows0"), sem("s_rows1")]
        gates_ready = sem("gates_ready")
        scaled_ready = sem("scaled_ready")
        gated = sem("gated")
        added = sem("added")
        dve_added = sem("dve_added")

        block = ctx.enter_context(nc.Block())

        def tile(n, k):
            return n * TILES + k

        def quad(m, k, q):
            return m * (TILES * QUADS) + (k * QUADS + q)

        unit = quad

        def pooled_tile(j, r):
            return (j, r + LEAD) if r + LEAD < TILES else (j + 1, r + LEAD - TILES)

        def scaled_unit(s, last):
            if last and s >= TAIL and s % 4 >= 2:
                return normed[:, s % 2].rearrange("p f x -> p (f x)")
            return scaled[:, s % 2, :]

        def dve_adds(s):
            return sum(d < s for d in DVE_ADDS)

        def gate_image(j, part):
            return j if part == LOW else j + 1

        def half_count(m, part):
            return 2 * m + part

        def quartered(k):
            return k % 4 != 3

        def quarters_before(k):
            return sum(quartered(i) for i in range(k))

        QUARTERED = quarters_before(TILES)

        OUT_ROWS = {UP: slice(0, H // 2), LOW: slice(H // 2, H)}
        IN_ROWS = {UP: slice(0, HALO), LOW: slice(0, H)}
        NEW_ROWS = {UP: slice(0, HALO), LOW: slice(H // 2, H)}
        NEW = {UP: HALO, LOW: H // 2}

        @block.sync
        def _(sp):
            with nc.allow_non_contiguous_dma(reason="a value for each channel"):
                sp.dma_start(col(BNW, 0, 2), bn_w.rearrange("(f p) -> p f", p=P)).then_inc(weights, 16)

            for k in range(TILES):
                sp.dma_start(image[:, k], x_t[0, k]).then_inc(loaded[k], 16)
            sp.wait_ge(lined, 1 + TAPS)
            sp.dma_start(via_lines, lines[0:BANDS, :]).then_inc(lines_out, 16)
            sp.wait_ge(lines_out, 16)
            skewed = bass.AP(via_lines.tensor, 0, [[1, P], [2 * P, BANDS], [1, P]])
            sp.dma_start(bands_flat, skewed).then_inc(banded, 16)
            with sp.Fori(1, N) as n:
                for k in range(TILES):
                    halves_done = tile(n - 1, k + 1) * HALVES
                    sp.wait_ge(squared, halves_done)
                    sp.wait_ge(max_step, halves_done)
                    sp.wait_ge(fold_ready, halves_done)
                    sp.wait_ge(h_summed, halves_done)
                    sp.dma_start(image[:, k], x_t[n, k]).then_inc(loaded[k], 16)

            sp.wait_ge(pools_kept, 16 * N)
            sp.dma_start(pools[:, :, :], kept[N - 1]).then_inc(pools_in, 16)
            sp.wait_ge(consts, CONSTS)

            def spread_gate_s(g):
                rows = pix[SROW:KROWS, g % 2, :].rearrange("a (r w) -> a r w", w=W)
                gate_s = via_s[g * GROWS:(g + 1) * GROWS].rearrange("r a w -> a r w")
                sp.dma_start(rows, gate_s).then_inc(s_rows[g % 2], 16)

            def leave_gates(m, part):
                sp.wait_ge(ws_split, (half_count(m, part) + 1) * SPLIT)
                rows = OUT_ROWS[part]
                for at, width, via, left in ((0, C // 2, via_w, w_left), (C // 2, W // 2, via_s, s_left)):
                    for b in range(2):
                        sp.dma_start(via[rows, :, b * width:(b + 1) * width],
                                     ws_parts[b * H // 2:(b + 1) * H // 2, :, at:at + width]).then_inc(left, 16)

            def stack_gates(m, part):
                sp.wait_ge(w_left, 32 * (half_count(m, part) + 1))
                groups = slice(part * GROUPS // 2, (part + 1) * GROUPS // 2)
                by_group = via_w.rearrange("(g r) a c -> a r g c", r=GROWS)
                for a in range(PARTS):
                    sp.dma_start(gw_stack[a * GROWS:(a + 1) * GROWS, groups, :], by_group[a, :, groups, :]
                                 ).then_inc(w_stacked, 16)
                sp.wait_ge(s_left, 32 * (half_count(m, part) + 1))
                spread_gate_s(part * GROUPS // 2)

            def step(j, here, after, first=False, last=False):
                if not last:
                    sp.wait_ge(z_scaled, (j + 1) * 3)
                    sp.dma_start(pools[:, :, :], kept[after]).then_inc(pools_in, 16)
                for r in range(TILES):
                    placing = r in PLACE and not (last and PLACE[r] == UP)
                    late = dve_adds(2 * r + 2) if last else 0
                    sp.wait_ge(added, unit(j, r + 1, 0) - late)
                    if late:
                        sp.wait_ge(dve_added, late)
                    sp.dma_start(out_t[here, r], image[:, r]).then_inc(stored[r], 16)
                    if r > 0 and not last:
                        sp.wait_ge(stored[r - 1], 16 * (j + 1))
                        sp.dma_start(image[:, r - 1], x_t[after, r - 1]).then_inc(loaded[r - 1], 16)
                    if r == 0 and not first:
                        sp.wait_ge(stored[TILES - 1], 16 * j)
                        sp.dma_start(image[:, TILES - 1], x_t[here, TILES - 1]).then_inc(loaded[TILES - 1], 16)
                    if placing:
                        leave_gates(gate_image(j, PLACE[r]), PLACE[r])
                        stack_gates(gate_image(j, PLACE[r]), PLACE[r])
                    if r in S_ROWS and not (last and S_ROWS[r] < 2):
                        spread_gate_s(S_ROWS[r])

            leave_gates(0, UP)
            stack_gates(0, UP)
            spread_gate_s(1)
            step(0, N - 1, 0, first=True)
            with sp.Fori(1, N - 1) as j:
                step(j, j - 1, j)
            step(N - 1, N - 2, None, last=True)
            for k in range(TILES):
                sp.wait_ge(stored[k], 16 * N)

        @block.gpsimd
        def _(pool):
            pool.memset(lines[:, :], 0.0).then_inc(lined, 1)
            pool.memset(ident[:, :], 0.0).then_inc(consts, 1)
            pool.memset(mirror[:, :], 0.0).then_inc(consts, 1)
            pool.memset(mean_strip[:, 0:COLS - 1], 0.0).then_inc(consts, 1)
            pool.memset(mean_strip[:, COLS - 1:COLS], 1.0 / C).then_inc(consts, 1)
            pool.memset(mean_strip[:, COLS:], 0.0).then_inc(consts, 1)
            pool.memset(cmax_t[:, :, :], 0.0).then_inc(consts, 1)
            pool.memset(zeros[:, :], 0.0).then_inc(consts, 1)
            for z in (z_h, z_w, z_s):
                pool.memset(z[:, :, :], 0.0).then_inc(consts, 1)
            pool.wait_ge(consts, IDENTS - 2)
            pool.affine_select(out=ident[:, :], in_=ident[:, :], compare_op=ALU.not_equal, fill=1.0, base=0,
                               pattern=[[-1, P]], channel_multiplier=1).then_inc(consts, 1)
            pool.affine_select(out=mirror[:, :], in_=mirror[:, :], compare_op=ALU.not_equal, fill=1.0,
                               base=1 - P, pattern=[[1, P]], channel_multiplier=1).then_inc(consts, 1)

            def make_lines():
                pool.wait_ge(lined, 1)
                pool.wait_ge(tapped, 16 * 5)
                for k in range(TAPS):
                    at = P - 1 - PAD + k
                    pool.tensor_copy(lines[0:BANDS, at:at + 1], taps_in[0:BANDS, k:k + 1]).then_inc(lined, 1)

            def one_hots():
                pool.memset(pix[:, :, :], 0.0).then_inc(consts, 1)
                pool.memset(gw_stack[:, :, :], 1.0).then_inc(consts, 1)
                pool.wait_ge(consts, IDENTS + 2)
                for part in range(PARTS):
                    for b in range(2):
                        rows = pix[:, b, :].rearrange("p (r w) -> p r w", w=W)
                        pool.affine_select(out=rows, in_=rows, compare_op=ALU.not_equal, fill=1.0,
                                           base=-part * GROWS, pattern=[[-1, GROWS], [0, W]],
                                           channel_multiplier=1).then_inc(consts, 1)
                    pool.wait_ge(consts, IDENTS + 2 + 2 * (part + 1))

            def sweep1(n, first=False):
                for k in range(TILES):
                    b = k % 2
                    if first and k == 3:
                        make_lines()
                    pool.wait_ge(loaded[k], 16 * (n + 1))
                    if not (first and k < 2):
                        pool.wait_ge(fold_used, tile(n, k) - 1)
                    px = image[:, k].rearrange("p f (r w) -> p f r w", w=W)
                    pool.tensor_tensor(folded[:, b], px[:, :, :, 0:W // 2], px[:, :, :, W // 2:W],
                                       ALU.add).then_inc(fold_ready, 2)
                    if quartered(k):
                        pool.wait_ge(fold_ready, tile(n, k + 1) * 2)
                        pool.tensor_tensor(folded2[:, b], folded[:, b, :, :, 0:W // 4],
                                           folded[:, b, :, :, W // 4:W // 2], ALU.add).then_inc(fold2_ready, 1)

            sweep1(0, True)
            with pool.Fori(1, N) as n:
                sweep1(n)

            def normalise_pool(m, n):
                a_all = a_row[:, 0:2, :].rearrange("p a q -> p (a q)")
                d_all = a_row[:, 2:4, :].rearrange("p a q -> p (a q)")
                z = (z_h[:, 1, PAD:PAD + C], z_h[:, 0, PAD:PAD + C], z_w[:, 1, PAD:PAD + C])[n]
                pool.tensor_tensor(z, pools[:, n, :], (a_row_w[:, :], a_all, a_row_w[:, :])[n], ALU.mult
                                   ).then_inc(z_scaled, 1)
                pool.wait_ge(z_scaled, 3 * m + n + 1)
                pool.tensor_tensor(z, z, d_all, ALU.add).then_inc(z_pooled, 1)

            def split(m, part, first=False):
                n = half_count(m, part)
                pool.wait_ge(ws_gate, 2 * (n + 1))
                if not first:
                    pool.wait_ge(w_left, 32 * n)
                    pool.wait_ge(s_left, 32 * n)
                for a in range(PARTS):
                    pool.tensor_tensor(ws_parts[:, a, :], gate_ws[:, :], zeros[:, :], ALU.add
                                       ).then_inc(ws_split, 1)
                    if a + 1 < PARTS:
                        pool.wait_ge(ws_split, SPLIT * n + 2 * a + 1)
                        pool.tensor_tensor(gate_ws[:, :], gate_ws[:, :], ws_parts[:, a, :], ALU.subtract
                                           ).then_inc(ws_split, 1)
                        pool.wait_ge(ws_split, SPLIT * n + 2 * a + 2)

            def add_x(j, s, last=False):
                r, f = divmod(s, 2)
                pool.wait_ge(gated, unit(j, r, f) + 1)
                pool.tensor_tensor(image[:, r, f, :], image[:, r, f, :], scaled_unit(s, last), ALU.add
                                   ).then_inc(added, 1)

            def steps(j, last=False):
                for s in range(2 * TILES):
                    if not (last and s in DVE_ADDS):
                        add_x(j, s, last)
                    if s in POOLS and not last:
                        if s == POOLS[0]:
                            pool.wait_ge(pools_in, 16 * (j + 2))
                            pool.wait_ge(ws_conv, half_count(j, LOW) + 1)
                        normalise_pool(j + 1, s - POOLS[0])
                    if s in SIGMOID and not (last and SIGMOID[s] == UP):
                        split(gate_image(j, SIGMOID[s]), SIGMOID[s])

            pool.wait_ge(rows_out, 2)
            pool.wait_ge(pools_in, 16)
            for n in range(3):
                normalise_pool(0, n)
            one_hots()
            split(0, UP, first=True)
            with pool.Fori(0, N - 1) as j:
                steps(j)
            steps(N - 1, last=True)

        @block.scalar
        def _(act):
            with nc.allow_non_contiguous_dma(reason="294 taps, a line for each band matrix; parameters"):
                act.dma_start(taps_in[0:2 * TAPS, :], w_h.rearrange("o i a b -> (o i a) b")).then_inc(tapped, 16)
                for g, src in ((1, w_w), (2, w_s)):
                    for i in range(2):
                        at = (g * 2 + i) * TAPS
                        act.dma_start(taps_in[at:at + TAPS, :], src[0, i].rearrange("a b -> b a")
                                     ).then_inc(tapped, 16)
                for g, src in enumerate((b_h, b_w, b_s, gamma)):
                    at = BIAS + g if g < 3 else G3
                    act.dma_start(small[:, at:at + 1], src.to_broadcast([P, 1])).then_inc(params, 16)
                act.dma_start(col(BNB, 0, 2), bn_b.rearrange("(f p) -> p f", p=P)).then_inc(params, 16)

            def sweep1(n, first=False):
                for k in range(TILES):
                    act.wait_ge(loaded[k], 16 * (n + 1))
                    for f in range(HALVES):
                        if not (first and k == 0 and f == 0):
                            act.wait_ge(squared, tile(n, k) * HALVES + f)
                        act.activation(square_junk, image[:, k, f, :], ACT.Square, bias=col(SHIFT, f),
                                       accum_out=squares[:, n, k, f:f + 1]).then_inc(squared, 1)
                act.wait_ge(pools_turned, n + 1)
                if not first:
                    act.wait_ge(pools_kept, 16 * n)
                act.activation(pools[:, 0, :], conv_ps[:, 0:C], ACT.Identity)
                act.activation(pools[:, 1:3, :].rearrange("p a c -> p (a c)"), csum_ps[:, :],
                               ACT.Identity).then_inc(pools_out, 1)
                act.wait_ge(pools_out, n + 1)
                act.dma_start(kept[n], pools[:, :, :]).then_inc(pools_kept, 16)

            act.wait_ge(shifted, 2)
            sweep1(0, True)
            for n in range(FLIPS):
                act.wait_ge(band_turned, n + 1)
                four = bands_flat[:, 4 * n:min(4 * n + 4, BANDS)].rearrange("p b q -> p (b q)")
                act.activation(four, turn_ps[n % 2][:, 0:four.shape[1]], ACT.Identity).then_inc(bands_ready, 1)
            with act.Fori(1, N) as n:
                sweep1(n)
            act.wait_ge(stat, VAR_STEPS)
            act.activation(col(RSTD, 0, 2), col(VAR, 0, 2), ACT.Sqrt).then_inc(rooted, 1)
            act.wait_ge(stat, STAT_STEPS)

            def normalise(m, k, q, first=False):
                if q == 0:
                    act.wait_ge(loaded[k], 16 * (N + m))
                if not (first and k == 0):
                    act.wait_ge(half_ready, quad(m, k, q) - 1)
                    act.wait_ge(c_summed, quad(m, k, q) - 1)
                for f in range(HALVES):
                    last = act.activation(normed[:, q, f, :], image[:, k, f, q * QPX:(q + 1) * QPX],
                                          ACT.Identity, scale=col(A, f), bias=col(D, f))
                last.then_inc(normed_ready, 1)

            def csum_leaves(m, part):
                act.wait_ge(c_summed, quad(m, TOP + 1 if part == UP else TILES, 0))
                if part == LOW:
                    act.wait_ge(ws_conv, half_count(m, part))
                act.activation(z_s[:, 1, PAD:PAD + W], csum_ps[:, 0:W], ACT.Identity).then_inc(csum_out, 1)

            def take_pools(m, part, first=False):
                act.wait_ge(pools_flat, half_count(m, part) + 1)
                if not first:
                    act.wait_ge(ws_conv, half_count(m, part))
                rows, new = NEW_ROWS[part], NEW[part]
                act.activation(z_w[rows, 0, PAD:PAD + C], conv_ps[0:new, 0:C], ACT.Identity).then_inc(z_ready, 1)
                act.activation(z_s[:, 0, PAD:PAD + W], conv_ps[:, C:C + W], ACT.Identity).then_inc(z_ready, 1)

            def scale(j, r, f, first=False, last=False):
                s = 2 * r + f
                before = s - 4 if last and s >= TAIL + 4 else s - 2
                if last and s in (TAIL + 2, TAIL + 3):
                    act.wait_ge(half_ready, quad(N, 0, 0))
                    act.wait_ge(c_summed, quad(N, 0, 0))
                elif last and before in DVE_ADDS:
                    act.wait_ge(dve_added, dve_adds(before) + 1)
                elif not first or before >= 0:
                    act.wait_ge(added, unit(j, 0, before) + 1 - (dve_adds(before) if last else 0))
                act.activation(scaled_unit(s, last), image[:, r, f, :], ACT.Identity,
                               scale=col(A3, f), bias=col(D3, f)).then_inc(scaled_ready, 1)

            def sigmoid_h(m, first=False):
                act.wait_ge(h_conv, m + 1)
                if not first:
                    act.wait_ge(h_gate, m)
                act.activation(gate_h_next, conv_ps[:, 0:C], ACT.Sigmoid, bias=col(BIAS, 0)
                               ).then_inc(h_sigmoid, 1)

            def pass_gate_h(m, first=False):
                act.wait_ge(h_sigmoid, m + 1)
                if not first:
                    act.wait_ge(gates_ready, unit(m, 0, 0))
                act.activation(gate_h, gate_h_next, ACT.Identity).then_inc(h_gate, 1)

            def sigmoids(m, part, first=False):
                n = half_count(m, part)
                act.wait_ge(ws_conv, n + 1)
                if not first:
                    act.wait_ge(ws_split, SPLIT * n)
                act.activation(gate_ws[:, 0:C // 2], conv_ps[:, 0:C // 2], ACT.Sigmoid,
                               bias=col(BIAS, 1)).then_inc(ws_gate, 1)
                act.activation(gate_ws[:, C // 2:], conv_ps[:, C // 2:(C + W) // 2], ACT.Sigmoid,
                               bias=col(BIAS, 2)).then_inc(ws_gate, 1)

            for k in range(LEAD):
                for q in range(QUADS):
                    normalise(0, k, q, True)
                if k == TOP - 1:
                    sigmoid_h(0, True)
                    pass_gate_h(0, True)
                if k == TOP:
                    csum_leaves(0, UP)
                    take_pools(0, UP, True)
                if k == TOP + 2:
                    sigmoids(0, UP, True)

            def steps(j, first=False, last=False):
                for s in range(2 * TILES):
                    r, n = divmod(s, 2)
                    m, k = pooled_tile(j, r)
                    if not (last and r + LEAD >= TILES):
                        normalise(m, k, n)
                    if s - 1 in SIGMOID and not (last and SIGMOID[s - 1] == UP):
                        sigmoids(gate_image(j, SIGMOID[s - 1]), SIGMOID[s - 1])
                    if s - 2 in TURN and not (last and TURN[s - 2] == UP):
                        take_pools(gate_image(j, TURN[s - 2]), TURN[s - 2])
                    scale(j, r, n, first, last)
                    if s in CSUM_OUT and not (last and CSUM_OUT[s] == UP):
                        csum_leaves(gate_image(j, CSUM_OUT[s]), CSUM_OUT[s])
                    if s == H_SIGMOID and not last:
                        sigmoid_h(j + 1)
                if not last:
                    pass_gate_h(j + 1)

            steps(0, first=True)
            with act.Fori(1, N - 1) as j:
                steps(j)
            steps(N - 1, last=True)

        @block.vector
        def _(dve):
            dve.wait_ge(weights, 16)
            dve.tensor_scalar(col(T0, 0, 2), col(BNW, 0, 2), 0.0, None, ALU.is_ge).then_inc(signed, 1)
            dve.wait_ge(signed, 1)
            dve.tensor_scalar(col(SIGN, 0, 2), col(T0, 0, 2), 2.0, -1.0, ALU.mult, ALU.add).then_inc(signed, 1)
            dve.wait_ge(signed, 2)

            dve.wait_ge(loaded[0], 16)
            dve.tensor_reduce(col(SHIFT, 0, 2), image[:, 0], AX.X, ALU.add).then_inc(shifted, 1)
            dve.wait_ge(shifted, 1)
            dve.tensor_scalar(col(SHIFT, 0, 2), col(SHIFT, 0, 2), -1.0 / TPX, None, ALU.mult
                              ).then_inc(shifted, 1)

            def sweep1(n, first=False):
                for k in range(TILES):
                    dve.wait_ge(loaded[k], 16 * (n + 1))
                    for f in range(HALVES):
                        if k == 0:
                            if not first:
                                dve.wait_ge(h_maxed, 2 * n)
                            op = dve.tensor_scalar(gates_ps[:, f, :], image[:, k, f, :], col(SIGN, f), None,
                                                   ALU.mult)
                        else:
                            dve.wait_ge(max_step, tile(n, k) * HALVES + f - 1)
                            op = dve.scalar_tensor_tensor(
                                out=gates_ps[:, f, :], in0=image[:, k, f, :], scalar=col(SIGN, f),
                                in1=gates_ps[:, f, :], op0=ALU.mult, op1=ALU.max)
                        op.then_inc(max_step, 1)
                    if not first and k == 0:
                        dve.wait_ge(pools_turned, n)
                    if quartered(k):
                        dve.wait_ge(fold2_ready, n * QUARTERED + quarters_before(k) + 1)
                        sums = folded2[:, k % 2]
                    else:
                        dve.wait_ge(fold_ready, tile(n, k + 1) * 2)
                        sums = folded[:, k % 2]
                    dve.tensor_reduce(wsum[:, :, k * ROWS:(k + 1) * ROWS], sums, AX.X, ALU.add
                                      ).then_inc(fold_used, 1)
                dve.wait_ge(max_step, tile(n, TILES) * HALVES)
                for f in range(HALVES):
                    last = dve.tensor_reduce(hmax_raw[:, f], gates_ps[:, f, :].rearrange(
                        "p (r w) -> p w r", w=W), AX.X, ALU.max)
                last.then_inc(h_maxed, 1)
                dve.wait_ge(fold_used, tile(n, TILES))
                dve.tensor_reduce(totals[:, n, :], wsum[:, :, :], AX.X, ALU.add).then_inc(h_maxed, 1)
                dve.wait_ge(h_maxed, 2 * n + 2)
                for f in range(HALVES):
                    last = dve.tensor_scalar(hmax[:, f], hmax_raw[:, f], col(SIGN, f), None, ALU.mult)
                last.then_inc(pools_ready, 1)

            sweep1(0, True)
            with dve.Fori(1, N) as n:
                sweep1(n)

            dve.wait_ge(params, 16 * 5)
            dve.wait_ge(squared, N * TILES * HALVES)
            dve.wait_ge(pools_turned, N)
            done = [0]

            def chain(op):
                done[0] += 1
                op.then_inc(stat, 1)
                dve.wait_ge(stat, done[0])

            two = lambda c: col(c, 0, 2)
            count = N * H * W
            chain(dve.tensor_reduce(two(MEAN), totals[:, :, :].rearrange("p n f -> p f n"), AX.X, ALU.add))
            chain(dve.tensor_reduce(two(VAR), squares[:, :, :, :].rearrange("p n t f -> p f (n t)"), AX.X,
                                    ALU.add))
            chain(dve.tensor_scalar(two(MEAN), two(MEAN), 1.0 / count, None, ALU.mult))
            chain(dve.tensor_tensor(two(T0), two(MEAN), two(SHIFT), ALU.add))
            chain(dve.tensor_tensor(two(T0), two(T0), two(T0), ALU.mult))
            chain(dve.tensor_scalar(two(VAR), two(VAR), 1.0 / count, BN_EPS, ALU.mult, ALU.add))
            chain(dve.tensor_tensor(two(VAR), two(VAR), two(T0), ALU.subtract))
            assert done[0] == VAR_STEPS
            dve.wait_ge(rooted, 1)
            chain(dve.reciprocal(two(T1), two(RSTD)))
            chain(dve.tensor_tensor(two(T2), two(T1), two(T1), ALU.mult))
            chain(dve.tensor_tensor(two(T2), two(T2), two(VAR), ALU.mult))
            chain(dve.tensor_scalar(two(T2), two(T2), -0.5, 1.5, ALU.mult, ALU.add))
            chain(dve.tensor_tensor(two(T1), two(T1), two(T2), ALU.mult))
            chain(dve.tensor_tensor(two(A), two(BNW), two(T1), ALU.mult))
            chain(dve.tensor_tensor(two(T0), two(MEAN), two(A), ALU.mult))
            chain(dve.tensor_tensor(two(D), two(BNB), two(T0), ALU.subtract))
            chain(dve.tensor_scalar(col(G3), col(G3), 1.0 / 3.0, None, ALU.mult))
            chain(dve.tensor_scalar(two(A3), two(A), col(G3), None, ALU.mult))
            chain(dve.tensor_scalar(two(D3), two(D), col(G3), None, ALU.mult))
            assert done[0] == STAT_STEPS
            dve.wait_ge(rows_turned, 1)
            dve.tensor_copy(a_row[:, :, :].rearrange("p a q -> p (a q)"), turn_ps[0][:, :]).then_inc(rows_out, 1)
            dve.tensor_scalar(a_row_w[:, :], turn_ps[0][:, 0:C], 1.0 / W, None, ALU.mult).then_inc(rows_out, 1)

            def pool_quad(m, k, q, first=False):
                dve.wait_ge(normed_ready, quad(m, k, q) + 1)
                if not first and q == 0 and k in (0, TOP):
                    dve.wait_ge(pools_flat, half_count(m, UP) - 1 + k // TOP)
                h0 = k * ROWS + q * QROWS
                dve.tensor_reduce(wmax[:, :, h0:h0 + QROWS],
                                  normed[:, q].rearrange("p f (r w) -> p f r w", w=W), AX.X, ALU.max)
                if not (first and k == 0):
                    dve.wait_ge(turned, quad(m, k, q) - 1)
                dve.tensor_tensor(halfmax[:, q, :], normed[:, q, 0, :], normed[:, q, 1, :],
                                  ALU.max).then_inc(half_ready, 1)

            def cmax_quad(m, k, q, first=False):
                dve.wait_ge(turned, quad(m, k, q) + 1)
                if (k, q) == (TOP, 1):
                    dve.wait_ge(pools_flat, half_count(m, UP) + 1)
                if not first and (k, q) == (0, 0):
                    dve.wait_ge(pools_flat, half_count(m, UP))
                dve.tensor_reduce(cmax_t[:, :, k * QUADS + q],
                                  turn_ps[q][:, :].rearrange("p (r c) -> p r c", c=P), AX.X, ALU.max
                                  ).then_inc(c_maxed, 1)

            def gate_unit(j, r, f, last=False):
                dve.wait_ge(gates_ready, unit(j, r, f) + 1)
                dve.wait_ge(scaled_ready, unit(j, r, f) + 1)
                unit_px = scaled_unit(2 * r + f, last)
                dve.tensor_tensor(unit_px, gates_ps[:, f, :], unit_px, ALU.mult).then_inc(gated, 1)

            for k in range(LEAD):
                for q in range(QUADS):
                    pool_quad(0, k, q, True)
                    if q == 1:
                        cmax_quad(0, k, 0, True)
                    elif k > 0:
                        cmax_quad(0, k - 1, 1)

            def steps(j, first=False, last=False):
                for s in range(2 * TILES):
                    r, n = divmod(s, 2)
                    m, k = pooled_tile(j, r)
                    if not (last and r + LEAD >= TILES):
                        pool_quad(m, k, n)
                    if not (last and s > 2 * (TILES - LEAD)):
                        if n == 0:
                            m, k = pooled_tile(j, r - 1)
                        cmax_quad(m, k, 1 - n)
                    gate_unit(j, r, n, last)
                    if last and s in DVE_ADDS:
                        dve.wait_ge(gated, unit(j, r, n) + 1)
                        dve.tensor_tensor(image[:, r, n, :], image[:, r, n, :], scaled_unit(s, last), ALU.add
                                          ).then_inc(dve_added, 1)

            steps(0, first=True)
            with dve.Fori(1, N - 1) as j:
                steps(j)
            steps(N - 1, last=True)

        @block.tensor
        def _(pe):
            pe.wait_ge(consts, IDENTS)

            def turn(dst, src, start=True, stop=True):
                return pe.matmul(dst, src, ident[:, :], start=start, stop=stop, is_transpose=True,
                                 skip_group_check=True)

            def sweep1(n, first=False):
                for k in range(TILES):
                    pe.wait_ge(loaded[k], 16 * (n + 1))
                    if not first and k == 0:
                        pe.wait_ge(pools_out, n)
                    for f in range(HALVES):
                        for r in range(ROWS):
                            last = turn(conv_ps[:, f * P:(f + 1) * P], image[:, k, f, r * W:(r + 1) * W],
                                        start=(k == 0 and f == 0 and r == 0),
                                        stop=(k == TILES - 1 and r == ROWS - 1))
                        last.then_inc(h_summed, 1)
                pe.wait_ge(pools_ready, n + 1)
                for f in range(HALVES):
                    turn(csum_ps[:, f * P:(f + 1) * P], hmax[:, f])
                for f in range(HALVES):
                    last = turn(csum_ps[:, C + f * P:C + (f + 1) * P], wsum[:, f])
                last.then_inc(pools_turned, 1)

            sweep1(0, True)
            pe.wait_ge(banded, 16)
            for n in range(FLIPS):
                if n >= 2:
                    pe.wait_ge(bands_ready, n - 1)
                for i, band in enumerate(range(4 * n, min(4 * n + 4, BANDS))):
                    groups = QROWS if band >= 2 * 2 * TAPS else 1
                    for g in range(groups):
                        rows = slice(g * P // groups, (g + 1) * P // groups)
                        last = pe.matmul(turn_ps[n % 2][rows, i * P:(i + 1) * P], bands_flat[:, band, g::groups],
                                         mirror[:, :], start=True, stop=True, is_transpose=groups == 1,
                                         skip_group_check=True, tile_position=(0, rows.start))
                last.then_inc(band_turned, 1)
            with pe.Fori(1, N) as n:
                sweep1(n)

            pe.wait_ge(stat, STAT_STEPS)
            for i, c in enumerate((A, A + 1, D, D + 1)):
                last = pe.matmul(turn_ps[0][:, i * P:(i + 1) * P], small[:, c:c + 1].to_broadcast([P, P]),
                                 ident[:, :], start=True, stop=True)
            last.then_inc(rows_turned, 1)
            pe.wait_ge(rows_out, 2)
            pe.wait_ge(bands_ready, FLIPS)

            def turn_quad(m, k, q, first=False):
                pe.wait_ge(half_ready, quad(m, k, q) + 1)
                if not (first and k == 0):
                    pe.wait_ge(c_maxed, quad(m, k, q) - 1)
                for r in range(QROWS):
                    last = turn(turn_ps[q][:, r * P:(r + 1) * P], halfmax[:, q, r * W:(r + 1) * W])
                last.then_inc(turned, 1)

            def csum_quad(m, k, q, first=False):
                pe.wait_ge(normed_ready, quad(m, k, q) + 1)
                at = k * QUADS + q
                window = mean_strip[:, COLS - 1 - at:2 * COLS - 1 - at]
                if (k, q) == (TOP + 1, 0):
                    pe.wait_ge(csum_out, half_count(m, UP) + 1)
                if not first and (k, q) == (0, 0):
                    pe.wait_ge(csum_out, half_count(m, UP))
                for f in range(HALVES):
                    for row in range(QROWS):
                        group = slice(COLS * row, COLS * (row + 1))
                        last = pe.matmul(csum_ps[group, 0:W], window, normed[:, q, f, row * W:(row + 1) * W],
                                         start=(at == 0 and f == 0), stop=(f == HALVES - 1),
                                         tile_position=(0, group.start), skip_group_check=True)
                last.then_inc(c_summed, 1)

            def convolve(rows_in, rows_out, rows_to, at, g, z, cols, tap):
                i, o = divmod(tap, TAPS)
                return pe.matmul(conv_ps[rows_to, at:at + cols.stop - cols.start], bands[rows_in, g, tap, rows_out],
                                 z[rows_in, i, cols.start + o:cols.stop + o],
                                 start=(tap == 0 and at == 0), stop=(tap == 2 * TAPS - 1),
                                 skip_group_check=True)

            def conv_h(m, taps, first=False):
                if taps[0] == 0:
                    pe.wait_ge(z_pooled, 3 * (m + 1))
                    if not first:
                        pe.wait_ge(ws_gate, 2 * half_count(m, UP))
                for tap in taps:
                    last = convolve(slice(0, P), slice(0, P), slice(0, P), 0, 0, z_h, slice(0, C), tap)
                if taps[-1] == 2 * TAPS - 1:
                    last.then_inc(h_conv, 1)

            def flatten_pools(m, part):
                if part == UP:
                    pe.wait_ge(h_sigmoid, m + 1)
                else:
                    pe.wait_ge(ws_gate, 2 * half_count(m, part))
                rows, new = NEW_ROWS[part], NEW[part]
                seen = quad(m, TOP, 1) if part == UP else quad(m, TILES, 0)
                pe.wait_ge(half_ready, seen)
                pe.wait_ge(c_maxed, seen)
                turn(conv_ps[:, C:C + W], cmax_t[:, :, :].rearrange("p g c -> p (g c)"))
                for f in range(HALVES):
                    last = turn(conv_ps[0:new, f * P:(f + 1) * P], wmax[:, f, rows])
                last.then_inc(pools_flat, 1)

            def conv_ws(m, part, taps):
                if taps[0] == 0:
                    pe.wait_ge(z_pooled, 3 * (m + 1))
                    pe.wait_ge(z_ready, 2 * (half_count(m, part) + 1))
                if taps[-1] >= TAPS:
                    pe.wait_ge(csum_out, half_count(m, part) + 1)
                for tap in taps:
                    for b in range(2):
                        convolve(IN_ROWS[part], OUT_ROWS[part], slice(b * H // 2, (b + 1) * H // 2), 0, 1,
                                 z_w, slice(b * C // 2, (b + 1) * C // 2), tap)
                    for b in range(2):
                        last = convolve(slice(0, P), OUT_ROWS[part], slice(b * H // 2, (b + 1) * H // 2), C // 2,
                                        2, z_s, slice(b * W // 2, (b + 1) * W // 2), tap)
                if taps[-1] == 2 * TAPS - 1:
                    last.then_inc(ws_conv, 1)

            def spread(j, r, f, first=False):
                g = r // GTILES
                if r == 0 and f == 0:
                    pe.wait_ge(h_gate, j + 1)
                if r in (0, TOP) and f == 0:
                    pe.wait_ge(w_stacked, 16 * PARTS * (half_count(j, r // TOP) + 1))
                if r % GTILES == 0 and f == 0:
                    pe.wait_ge(s_rows[g % 2], 16 * (j * (GROUPS // 2) + g // 2 + 1))
                if not (first and r == 0):
                    pe.wait_ge(gated, unit(j, r, f) - 1)
                for q in range(QUADS):
                    px = (r % GTILES) * TPX + q * QPX
                    dst = gates_ps[:, f, q * QPX:(q + 1) * QPX]
                    pe.matmul(dst, gw_stack[0:KROWS, g, f * P:(f + 1) * P], pix[0:KROWS, g % 2, px:px + QPX],
                              start=True, stop=False, skip_group_check=True)
                    for row in range(QROWS):
                        last = turn(dst[:, row * W:(row + 1) * W], gate_h[:, f * P:(f + 1) * P], start=False,
                                    stop=(row == QROWS - 1))
                last.then_inc(gates_ready, 1)

            for k in range(LEAD):
                for q in range(QUADS):
                    csum_quad(0, k, q, True)
                    turn_quad(0, k, q, True)
                if 2 <= k < 2 + len(H_CONV):
                    conv_h(0, H_CONV[min(H_CONV) + k - 2], True)
                if k == TOP:
                    flatten_pools(0, UP)
                    conv_ws(0, UP, range(TAPS))
                if k == TOP + 1:
                    conv_ws(0, UP, range(TAPS, 2 * TAPS))
            pe.wait_ge(consts, CONSTS)
            spread(0, 0, 0, True)

            def steps(j, first=False, last=False):
                for s in range(2 * TILES):
                    r, n = divmod(s, 2)
                    m, k = pooled_tile(j, r)
                    turning = s in TURN and not (last and TURN[s] == UP)
                    if not (last and r + LEAD >= TILES):
                        csum_quad(m, k, n)
                        turn_quad(m, k, n)
                    if s + 1 < 2 * TILES:
                        spread(j, (s + 1) // 2, (s + 1) % 2, first)
                    elif not last:
                        spread(j + 1, 0, 0)
                    if turning:
                        flatten_pools(gate_image(j, TURN[s]), TURN[s])
                    if s in CONV and not (last and CONV[s][0] == UP):
                        part, taps = CONV[s]
                        conv_ws(gate_image(j, part), part, taps)
                    if s in H_CONV and not last:
                        conv_h(j + 1, H_CONV[s])

            steps(0, first=True)
            with pe.Fori(1, N - 1) as j:
                steps(j)
            steps(N - 1, last=True)


_INS = {
    "x": "x", "bn_w": "L0_conv_bn_w", "bn_b": "L0_conv_bn_b", "w_h": "L0_conv_wH", "b_h": "L0_conv_bH",
    "w_w": "L0_conv_wW", "b_w": "L0_conv_bW", "w_s": "L0_conv_wS", "b_s": "L0_conv_bS",
    "gamma": "L0_conv_gamma",
}


def build(nc, arrays):
    args = {}
    for short, a in arrays.items():
        args[short] = nc.dram_tensor(f"in_{short}", a.shape, mybir.dt.from_np(a.dtype), kind="ExternalInput").ap()
    out = nc.dram_tensor("out_0", arrays["x"].shape, F32, kind="ExternalOutput").ap()
    triple_gate_kernel(nc, **args, out=out)


def kernel(**inputs):
    import numpy as np
    import concourse.bacc as bacc
    from concourse.bass_utils import run_bass_kernel_spmd

    nc = bacc.Bacc("TRN2", target_bir_lowering=False, num_devices=1)
    arrays = {}
    for short, name in _INS.items():
        a = np.ascontiguousarray(inputs[name])
        arrays[short] = a.reshape(a.shape or (1,))
    build(nc, arrays)
    r = run_bass_kernel_spmd(nc, [{f"in_{k}": v for k, v in arrays.items()}], core_ids=[0])
    return r.results[0]["out_0"]
```
